# Optimizing a Trainium2 kernel written in Bass

```python
import numpy as np
import jax
import jax.numpy as jnp

def _softmax(x, axis=-1):
    return jax.nn.softmax(x, axis=axis)
def _gelu(x):
    return jax.nn.gelu(x, approximate=True)
def _silu(x):
    return jax.nn.silu(x)
def _sigmoid(x):
    return jax.nn.sigmoid(x)
def _layernorm(x, axis=-1, eps=1e-5):
    m = jnp.mean(x, axis=axis, keepdims=True)
    v = jnp.var(x, axis=axis, keepdims=True)
    return (x - m) / jnp.sqrt(v + eps)
def _scatter_add(tgt, idx, src, axis=0):
    return tgt.at[idx].add(src)
def _segment_sum(src, seg, n):
    return jax.ops.segment_sum(src, seg, n)

kernel_name = 'mk_adj_resnorm_d1_adj_128_743029'

def setup_inputs(seed: int = 0):
    np.random.seed(seed)
    _w = jnp.asarray
    def _rec_inputs():
        import jax
        import jax.numpy as jnp
        _gk = jax.random.key(seed)
        x = -0.000929 + 1 * jax.random.normal(jax.random.fold_in(_gk, 1), (8192, 128), jnp.float32)
        _a = jax.random.bernoulli(jax.random.fold_in(_gk, 2), 0.00195312, (8192, 8192))
        _a = jnp.logical_or(_a, jnp.swapaxes(_a, -1, -2))
        _a = jnp.logical_or(_a, jnp.eye(8192, dtype=bool))
        adj = _a.astype(jnp.int32)
        return x, adj
    x, adj = _rec_inputs()
    def _L0_gnn_setup():
        import jax, jax.numpy as jnp
        import numpy as np
        N = 8192
        IN = 128
        OUT = 128
        THR = 0.0001
        ALPHA = 0.2
        NEG = -1000000000.0
        key = jax.random.key(seed)
        k1, k2, k3, k4 = jax.random.split(key, 4)
        inp = jax.random.normal(k1, (N, IN), jnp.float32)
        W = jax.random.normal(k2, (IN, OUT), jnp.float32) * (1.414 * np.sqrt(2.0 / (IN + OUT)))
        a = jax.random.normal(k3, (2 * OUT, 1), jnp.float32) * (1.414 * np.sqrt(2.0 / (2 * OUT + 1)))
        adj = jax.random.randint(k4, (N, N), 0, 2, jnp.int32)
        return {'input': inp, 'W': W, 'a': a, 'adj': adj, 'M': N}
    _L0_gnn_all = _L0_gnn_setup()
    _L0_gnn_in = {k: v for k, v in _L0_gnn_all.items() if k in ('W', 'a', )}
    del _L0_gnn_all

    return {
        "x": x,
        "adj": adj,
        "L0_gnn_W": _L0_gnn_in["W"],
        "L0_gnn_a": _L0_gnn_in["a"],
    }

def reference(x, adj, L0_gnn_W, L0_gnn_a):
    import jax
    import jax.numpy as jnp
    def _L0_gnn_ref(input, W, a, adj, M):
        import jax, jax.numpy as jnp
        import numpy as np
        N = 8192
        IN = 128
        OUT = 128
        THR = 0.0001
        ALPHA = 0.2
        NEG = -1000000000.0
        h = input @ W
        a_src = a[:OUT, 0]
        a_dst = a[OUT:, 0]
        e = jax.nn.leaky_relu((h[:M] @ a_src)[:, None] + (h @ a_dst)[None, :], negative_slope=ALPHA)
        valid = (adj[:M] > 0) & (h.sum(axis=1) != 0)[None, :]
        att = jax.nn.softmax(jnp.where(valid, e, NEG), axis=1)
        att = jnp.where(valid, att, 0.0)
        L = valid.sum(axis=1).astype(h.dtype)
        top = att.max(axis=1)
        attention = jnp.where(att >= THR, att, 0.0) * L[:, None]
        attention = jnp.where((top > THR)[:, None], attention, 0.0)
        h_prime = attention @ h
        return jax.nn.elu(h[:M] + h_prime)

    x = _layernorm(x + _L0_gnn_ref(x, L0_gnn_W, L0_gnn_a, adj, 8192), axis=-1)
    return x


_drawn_inputs = setup_inputs


def setup_inputs(seed=0):
    import zlib

    import numpy as np

    out = dict(_drawn_inputs(seed))
    spreads = {}
    factors = {}
    for name, (base, spread) in spreads.items():
        noise = np.random.default_rng([zlib.crc32(name.encode()), seed]).standard_normal(out[name].shape)
        drawn = base * np.exp(spread * noise) if base else spread * noise
        out[name] = jnp.asarray(drawn.astype(out[name].dtype))
    for name, factor in factors.items():
        out[name] = (out[name] * factor).astype(out[name].dtype)
    return out
```

```python
from contextlib import ExitStack

import numpy as np
import concourse.bass as bass
from concourse import mybir

P = 128
N = 8192
F = 128
BI = 512
NB = N // BI
TB = BI // P
CH = 4
NG = N // (P * CH)
NC = N // P
GW = CH * BI
HALF = GW // 2
NADJ = 4
RT = 4
DVE_CHUNKS = 1
XP = 2 * BI
NXP = N // XP

THR = 1e-4
SLOPE = 0.2
EPS = 1e-5
SHIFT = 32.0
BIG = float(2 ** 60)
ONE = 56.0
TINY = 1e-37
LN2 = float(np.log(2.0))
LNTHR = float(np.log(THR))
SM = 32
ROW_STEPS = 9


def graph_attention(nc, x, xT, W, WT, a_cols, adjT, ident, sel, out):
    fp32, bf16, u8, u32, i32 = (mybir.dt.float32, mybir.dt.bfloat16, mybir.dt.uint8, mybir.dt.uint32,
                                mybir.dt.int32)
    fp8 = mybir.dt.float8e4
    ALU = mybir.AluOpType
    ACT = mybir.ActivationFunctionType
    AX = mybir.AxisListType
    ds = bass.ds

    s_dram = nc.dram_tensor("s_rows", (NB, 1, BI), fp32).ap()
    x_blocks = x.rearrange("(n t p) f -> n p t f", t=TB, p=P)
    out_blocks = out.rearrange("(n t p) f -> n p t f", t=TB, p=P)
    xT_blocks = xT.rearrange("f (n i) -> n f i", i=BI)

    with ExitStack() as ctx:
        def sb(name, shape, dt):
            return ctx.enter_context(nc.sbuf_tensor(name, shape, dt))

        def ps(name):
            return ctx.enter_context(nc.psum_tensor(name, [P, BI], fp32))

        def sem(name):
            return ctx.enter_context(nc.semaphore(name))

        V = sb("V", [P, NG, GW], u8)
        U = sb("U", [P, NG, GW], u8)
        adj = sb("adj", [P, NADJ, HALF], i32)
        upper = sb("upper", [P, 2, GW], u8)
        above = sb("above", [P, 2, GW], u8)
        T0 = sb("T0", [P, GW], u8)
        T1 = sb("T1", [P, RT, GW], u8)
        T2 = sb("T2", [P, RT, GW], u8)
        WB = sb("WB", [P, NC, 2, F], bf16)
        WD = sb("WD", [P, NC, 2, F], bf16)
        h_all = WD[:].rearrange("p c t f -> p (c t f)").bitcast(fp32).rearrange("p (c f) -> p c f", f=F)
        WV = sb("WV", [P, NC, SM], bf16)
        WU = sb("WU", [P, NC, SM], bf16)
        s_row = sb("s_row", [P, BI], fp32)
        stat_sb = sb("stat_sb", [P, BI], fp32)
        diag = sb("diag", [P, TB, P], fp32)
        accS = sb("accS", [P, 2, BI], fp32)
        E1 = sb("E1", [P, TB, F], fp32)
        E2 = sb("E2", [P, TB, F], fp32)
        E3 = sb("E3", [P, TB, F], fp32)
        E4 = sb("E4", [P, TB, F], fp32)
        xN = sb("xN", [P, TB, F], fp32)
        xTb = sb("xTb", [P, BI], fp32)
        W_sb = sb("W_sb", [P, F], fp32)
        WT_sb = sb("WT_sb", [P, F], fp32)
        a_sb = sb("a_sb", [P, 3], fp32)
        wa_sb = sb("wa_sb", [P, 3], fp32)
        id_sb = sb("id_sb", [P, P], fp32)
        ones = sb("ones", [P, P], fp32)
        sel_sb = sb("sel_sb", [P, 3], fp32)
        sdz = sb("sdz", [P, NC, 3], fp32)
        valid = sb("valid", [P, NC], fp32)
        dmask = sb("dmask", [P, NC], fp32)
        dtop = sb("dtop", [P, 1], fp32)
        dmax = sb("dmax", [P, 1], fp32)
        dneg = sb("dneg", [P, NC], fp32)
        dbig = sb("dbig", [P, NC], fp32)
        sc = sb("sc", [P, NC], fp32)
        argB, argA, argC = (diag[:, 0, k * NC:(k + 1) * NC] if k < 2 else diag[:, 1, 0:NC] for k in range(3))
        mrow = sb("mrow", [P, NC], fp32)
        mthr = sb("mthr", [P, NC], fp32)
        At = sb("At", [P, NC], fp32)
        Bt = sb("Bt", [P, NC], fp32)
        Ct = sb("Ct", [P, NC], fp32)
        Dt = sb("Dt", [P, NC], fp32)
        rest = sb("rest", [P, 2, NC], fp32)
        FA = sb("FA", [P, NC], fp32)
        FC = sb("FC", [P, NC], fp32)
        sT = sb("sT", [NC, P], fp32)
        small = sb("small", [P, 12, TB], fp32)
        bn = sb("bn", [P, TB, 6], fp32)
        mv = sb("mv", [P, TB, 2], fp32)
        vareps = sb("vareps", [P, TB], fp32)
        rstd = sb("rstd", [P, TB], fp32)
        minus_half = sb("minus_half", [P, TB], fp32)

        accA, accC, stat, misc, thr, trA, trC, hh = [
            ps(x) for x in ("accA", "accC", "stat", "misc", "thr", "trA", "trC", "hh")]
        sdz_ps = misc[:, 0:3 * NC].rearrange("p (c q) -> p c q", q=3)
        row_ps = misc[:, 192:192 + 3 * TB].rearrange("p (t q) -> p t q", q=3)
        wa_ps = misc[:, 208:211]
        sT_ps = misc[0:NC, 256:256 + P]

        consts_loaded = sem("consts_loaded")
        xT_loaded = [sem(f"xT_loaded{k}") for k in range(NADJ)]
        adj_loaded = [sem(f"adj_loaded{k}") for k in range(NADJ)]
        s_loaded = sem("s_loaded")
        xb_loaded = sem("xb_loaded")
        s_stored = sem("s_stored")
        out_stored = sem("out_stored")
        passed = sem("passed")
        setup_done = sem("setup_done")
        wa_ready = sem("wa_ready")
        wa_copied = sem("wa_copied")
        h_ready = sem("h_ready")
        h_copied = sem("h_copied")
        top_ready = sem("top_ready")
        max_ready = sem("max_ready")
        tab_step = sem("tab_step")
        args_ready = sem("args_ready")
        exps_ready = sem("exps_ready")
        sT_ready = sem("sT_ready")
        sT_copied = sem("sT_copied")
        dbig_ready = sem("dbig_ready")
        stat_weights = sem("stat_weights")
        prod_ready = sem("prod_ready")
        hi_ready = sem("hi_ready")
        lo_ready = sem("lo_ready")
        adj_used = sem("adj_used")
        upper_ready = sem("upper_ready")
        upper_dve = sem("upper_dve")
        masks_ready = sem("masks_ready")
        stats_done = sem("stats_done")
        stat_copied = sem("stat_copied")
        rows_ready = sem("rows_ready")
        dve_step = sem("dve_step")
        mant_ready = sem("mant_ready")
        ln_ready = sem("ln_ready")
        diag_ready = sem("diag_ready")
        thr_ready = sem("thr_ready")
        factors_ready = sem("factors_ready")
        above_ready = sem("above_ready")
        t1_done = sem("t1_done")
        t2_done = sem("t2_done")
        main_done = sem("main_done")
        acc_copied = sem("acc_copied")
        tr_done = sem("tr_done")
        scaled = sem("scaled")
        y_parts = sem("y_parts")
        xm_done = sem("xm_done")
        ysum = sem("ysum")
        y_ready = sem("y_ready")
        ex_ready = sem("ex_ready")
        r_ready = sem("r_ready")
        r2_ready = sem("r2_ready")
        bn_part = sem("bn_part")
        bn_ready = sem("bn_ready")
        ve_ready = sem("ve_ready")
        rstd_ready = sem("rstd_ready")
        out_ready = sem("out_ready")

        def words(ap):
            return ap.bitcast(u32)

        def wait(eng, semaphore, value):
            if not isinstance(value, int) or value > 0:
                eng.wait_ge(semaphore, value)

        def hold(eng):
            eng.sem_inc(passed, 1)

        def rows(tab, n):
            return tab[:, ds(n * TB, TB)]

        def over_features(col):
            return col.unsqueeze(2).to_broadcast([P, TB, F])

        block = ctx.enter_context(nc.Block())

        @block.sync
        def _(sp):
            for dst, src in ((W_sb, W), (WT_sb, WT), (a_sb[:, 0:2], a_cols), (id_sb, ident), (sel_sb, sel)):
                sp.dma_start(dst[:] if dst is not a_sb else dst, src).then_inc(consts_loaded, 16)
            sp.dma_start(xTb[:], xT_blocks[0]).then_inc(consts_loaded, 16)
            sp.sem_inc(out_stored, 16)
            for q in range(NXP):
                wait(sp, h_ready, 2 * (q - NADJ + 1))
                sp.dma_start(adj[:, q % NADJ, :].bitcast(fp32), xT[:, q * XP:(q + 1) * XP]).then_inc(
                    xT_loaded[q % NADJ], 16)

            def load_adj(n, g):
                for half in range(2):
                    u = 2 * g + half
                    wait(sp, adj_used, n * 2 * NG + u - NADJ + 1)
                    hold(sp)
                    sp.dma_start(adj[:, u % NADJ, :], adjT[n, g, :, half, :]).then_inc(adj_loaded[u % NADJ], 16)

            def load_s(n):
                sp.dma_start(s_row[:], s_dram[n].to_broadcast([P, BI])).then_inc(s_loaded, 16)

            def step(n, first=False, last=False):
                if not last:
                    wait(sp, upper_ready, (n + 1) * NG)
                    wait(sp, masks_ready, (n + 1) * NG)
                    hold(sp)
                    load_s(n + 1)
                for g in range(NG):
                    if not last:
                        load_adj(n + 1, g)
                    if g == 8:
                        if not first:
                            wait(sp, out_ready, n)
                            hold(sp)
                            sp.dma_start(out_blocks[n - 1], E4[:]).then_inc(out_stored, 16)
                            wait(sp, tr_done, n)
                            wait(sp, xm_done, n)
                            hold(sp)
                        sp.dma_start(xN[:], x_blocks[n]).then_inc(xb_loaded, 16)
                        sp.dma_start(xTb[:], xT_blocks[n]).then_inc(xb_loaded, 16)

            wait(sp, h_ready, 2 * NXP)
            for g in range(NADJ // 2):
                load_adj(0, g)
            sp.wait_ge(sT_copied, 1)
            sp.dma_start(s_dram.rearrange("n o (t p) -> (n o t) p", p=P), sT[:]).then_inc(s_stored, 16)
            sp.wait_ge(s_stored, 16)
            load_s(0)
            for g in range(NADJ // 2, NG):
                load_adj(0, g)
            step(0, first=True)
            with sp.Fori(1, NB - 1) as n:
                step(n)
            step(NB - 1, last=True)
            sp.wait_ge(out_ready, NB)
            sp.dma_start(out_blocks[NB - 1], E4[:]).then_inc(out_stored, 16)
            sp.wait_ge(out_stored, 16 * (NB + 1))

        @block.tensor
        def _(pe):
            pe.wait_ge(consts_loaded, 6 * 16)
            pe.wait_ge(setup_done, 1)
            nc.tensor.matmul(wa_ps, WT_sb[:], a_sb[:], start=True, stop=True).then_inc(wa_ready, 1)
            pe.wait_ge(wa_copied, 1)
            for q in range(2 * NXP):
                bank = (trA, trC)[q % 2]
                if q % 2 == 0:
                    pe.wait_ge(xT_loaded[(q // 2) % NADJ], 16 * ((q // 2) // NADJ + 1))
                wait(pe, h_copied, q - 1)
                for t in range(TB):
                    c = q * TB + t
                    xt = adj[:, (q // 2) % NADJ, :].bitcast(fp32)[:, (c % (2 * TB)) * P:(c % (2 * TB) + 1) * P]
                    nc.tensor.matmul(bank[:, t * F:(t + 1) * F], xt, W_sb[:], start=True, stop=True)
                    last = nc.tensor.matmul(sdz_ps[:, c, :], xt, wa_sb[:], start=True, stop=True)
                last.then_inc(h_ready, 1)
            pe.wait_ge(tab_step, 1)
            nc.tensor.transpose(sT_ps, sdz[:, :, 0], id_sb[:]).then_inc(sT_ready, 1)

            def stats(n, g):
                if g == 0:
                    wait(pe, stat_copied, n)
                wait(pe, masks_ready, n * NG + g + 1)
                hold(pe)
                for masks, weights in ((V, WV), (U, WU)):
                    for c in range(CH):
                        last = nc.tensor.matmul(stat[c * SM:(c + 1) * SM, :], weights[:, g * CH + c, :],
                                                masks[:, g, c * BI:(c + 1) * BI].bitcast(fp8),
                                                start=(g == 0 and masks is V), stop=(g == NG - 1 and masks is U),
                                                tile_position=(0, c * SM))
                if g == NG - 1:
                    last.then_inc(stats_done, 1)

            def rows_and_threshold(n):
                wait(pe, stat_copied, n + 1)
                hold(pe)
                for t in range(TB):
                    last = nc.tensor.matmul(row_ps[:, t, :], stat_sb[:, t * P:(t + 1) * P], sel_sb[:],
                                            start=True, stop=True)
                last.then_inc(rows_ready, 1)
                wait(pe, diag_ready, n + 1)
                hold(pe)
                nc.tensor.matmul(thr[:], ones[:], diag[:].rearrange("p t i -> p (t i)"),
                                 start=True, stop=True).then_inc(thr_ready, 1)

            def main(n, g):
                if g == 0:
                    wait(pe, acc_copied, 2 * n)
                pe.wait_ge(lo_ready, g + 1)
                wait(pe, t2_done, n * NG + g + 1)
                hold(pe)
                for acc, masks, weights in ((accA, T1, WB), (accC, T2, WD)):
                    for c in range(CH):
                        for part in range(2):
                            last = nc.tensor.matmul(
                                acc[:], weights[:, g * CH + c, part, :],
                                masks[:, g % RT, c * BI:(c + 1) * BI].bitcast(fp8),
                                start=(g == 0 and c == 0 and part == 0),
                                stop=(g == NG - 1 and c == CH - 1 and part == 1))
                last.then_inc(main_done, 1)

            def to_rows(k):
                wait(pe, acc_copied, 2 * (k + 1))
                wait(pe, xb_loaded, 32 * (k + 1))
                hold(pe)
                for t in range(TB):
                    tile = slice(t * P, (t + 1) * P)
                    nc.tensor.transpose(trA[:, tile], accS[:, 0, tile], id_sb[:])
                    nc.tensor.transpose(trC[:, tile], accS[:, 1, tile], id_sb[:])
                    last = nc.tensor.matmul(hh[:, tile], xTb[:, tile], W_sb[:], start=True, stop=True)
                last.then_inc(tr_done, 1)

            def step(n, first=False, last=False):
                for g in range(NG):
                    if not last:
                        stats(n + 1, g)
                    main(n, g)
                    if g == 0 and not first:
                        to_rows(n - 1)
                if not last:
                    rows_and_threshold(n + 1)

            pe.wait_ge(stat_weights, 1)
            for g in range(NG):
                stats(0, g)
            rows_and_threshold(0)
            step(0, first=True)
            with pe.Fori(1, NB - 1) as n:
                step(n)
            step(NB - 1, last=True)
            to_rows(NB - 1)

        @block.scalar
        def _(act):
            for q in range(2 * NXP):
                act.wait_ge(h_ready, q + 1)
                nc.scalar.copy(h_all[:, q * TB:(q + 1) * TB, :],
                               (trA, trC)[q % 2][:].rearrange("p (t f) -> p t f", f=F)).then_inc(h_copied, 1)
            act.wait_ge(sT_ready, 1)
            nc.scalar.copy(sT[:], sT_ps).then_inc(sT_copied, 1)
            act.wait_ge(args_ready, 1)
            nc.scalar.activation(Bt[:], argB, ACT.Exp)
            nc.scalar.activation(Dt[:], argB, ACT.Exp, scale=SLOPE)
            nc.scalar.activation(At[:], argA, ACT.Exp)
            nc.scalar.activation(Ct[:], argC, ACT.Exp).then_inc(exps_ready, 1)

            def test_upper(n, g):
                if g == 0:
                    wait(act, s_loaded, 16 * (n + 1))
                wait(act, masks_ready, n * NG + g - 1)
                hold(act)
                for c in range(DVE_CHUNKS, CH):
                    last = nc.scalar.activation(upper[:, g % 2, c * BI:(c + 1) * BI].bitcast(fp8), s_row[:],
                                                ACT.Relu, scale=BIG, bias=dbig[:, g * CH + c:g * CH + c + 1],
                                                saturate=False)
                last.then_inc(upper_ready, 1)

            def test_above(n, g):
                if g == 0:
                    wait(act, thr_ready, n + 1)
                wait(act, t1_done, n * NG + g - 1)
                hold(act)
                for c in range(CH):
                    last = nc.scalar.activation(above[:, g % 2, c * BI:(c + 1) * BI].bitcast(fp8), thr[:],
                                                ACT.Relu, scale=-BIG, bias=dbig[:, g * CH + c:g * CH + c + 1],
                                                saturate=False)
                last.then_inc(above_ready, 1)

            def high_parts(g):
                act.wait_ge(prod_ready, g + 1)
                for dst, src in ((WB, (E1, E2)[g % 2]), (WD, (E3, E4)[g % 2])):
                    last = nc.scalar.copy(dst[:, g * CH:(g + 1) * CH, 0, :], src[:])
                last.then_inc(hi_ready, 1)

            def copy_sums(n):
                wait(act, stats_done, n + 1)
                nc.scalar.copy(stat_sb[:], stat[:]).then_inc(stat_copied, 1)

            def log_mantissa(n):
                wait(act, mant_ready, n + 1)
                nc.scalar.activation(small[:, 6, :], small[:, 5, :], ACT.Ln).then_inc(ln_ready, 1)

            def copy_acc(n):
                wait(act, main_done, (n + 1) * NG)
                for side, acc in enumerate((accA, accC)):
                    wait(act, tr_done, n)
                    nc.scalar.copy(accS[:, side, :], acc[:]).then_inc(acc_copied, 1)

            def exp_negative(k):
                wait(act, y_ready, k + 1)
                nc.scalar.activation(E3[:], E2[:], ACT.Exp).then_inc(ex_ready, 1)

            def step(n, first=False, last=False):
                if not last:
                    test_upper(n + 1, 0)
                for g in range(NG):
                    test_above(n, g)
                    if not last and g + 1 < NG:
                        test_upper(n + 1, g + 1)
                    if g == 2 and not first:
                        exp_negative(n - 1)
                if not last:
                    copy_sums(n + 1)
                    log_mantissa(n + 1)
                copy_acc(n)

            act.wait_ge(dbig_ready, 1)
            for g in range(NG):
                test_upper(0, g)
                high_parts(g)
            copy_sums(0)
            log_mantissa(0)
            step(0, first=True)
            with act.Fori(1, NB - 1) as n:
                step(n)
            step(NB - 1, last=True)
            exp_negative(NB - 1)

        @block.vector
        def _(dve):
            vec = nc.vector
            dve.wait_ge(wa_ready, 1)
            vec.tensor_copy(wa_sb[:], wa_ps).then_inc(wa_copied, 1)
            dve.wait_ge(h_ready, 2 * NXP)
            done = [0]

            def after(ins):
                ins.then_inc(tab_step, 1)
                done[0] += 1
                dve.wait_ge(tab_step, done[0])

            after(vec.tensor_copy(sdz[:], sdz_ps))
            s_tab, d_tab = sdz[:, :, 0], sdz[:, :, 1]
            vec.tensor_scalar(dneg[:], d_tab, -1.0, None, ALU.mult)
            vec.tensor_scalar(dbig[:], d_tab, BIG, None, ALU.mult).then_inc(dbig_ready, 1)
            after(vec.tensor_scalar(valid[:], sdz[:, :, 2], 0.0, None, ALU.not_equal))
            after(vec.tensor_scalar(rest[:, 0, :], valid[:], 1.0, 1e30, ALU.subtract, ALU.mult))
            after(vec.tensor_tensor(dmask[:], rest[:, 0, :], d_tab, ALU.add))
            vec.reduce_max(dtop[:], dmask[:], AX.X).then_inc(top_ready, 1)
            dve.wait_ge(max_ready, 1)
            after(vec.tensor_scalar(argB, d_tab, dmax[:, 0:1], 0.0, ALU.subtract, ALU.min))
            after(vec.tensor_scalar(argB, argB, SHIFT, None, ALU.add))
            after(vec.tensor_scalar(sc[:], s_tab, dmax[:, 0:1], None, ALU.add))
            after(vec.scalar_tensor_tensor(mrow[:], sc[:], SLOPE, sc[:], ALU.mult, ALU.max))
            vec.tensor_scalar(mthr[:], mrow[:], LNTHR, None, ALU.add)
            after(vec.tensor_scalar(sc[:], sc[:], -SHIFT, None, ALU.add))
            vec.tensor_tensor(argA, sc[:], mrow[:], ALU.subtract)
            vec.scalar_tensor_tensor(argC, sc[:], SLOPE, mrow[:], ALU.mult, ALU.subtract).then_inc(args_ready, 1)
            dve.wait_ge(exps_ready, 1)
            vec.tensor_tensor(Bt[:], Bt[:], valid[:], ALU.mult)
            after(vec.tensor_tensor(Dt[:], Dt[:], valid[:], ALU.mult))
            dve.wait_ge(setup_done, 1)
            after(vec.tensor_copy(WV[:, :, 6], valid[:]))
            for tab, first_col, side in ((Bt, 0, WU), (Dt, 3, WV)):
                src = tab[:]
                for part in range(3):
                    after(vec.tensor_copy(side[:, :, first_col + part], src))
                    if part < 2:
                        after(vec.tensor_tensor(rest[:, part, :], src, side[:, :, first_col + part], ALU.subtract))
                        src = rest[:, part, :]
            vec.tensor_scalar(WU[:, :, 3:6], WV[:, :, 3:6], -1.0, None, ALU.mult).then_inc(stat_weights, 1)

            def products(g):
                wait(dve, lo_ready, g - 1)
                h4 = h_all[:, g * CH:(g + 1) * CH, :]
                cols = slice(g * CH, (g + 1) * CH)
                vec.tensor_tensor((E1, E2)[g % 2][:], h4, over_features(Bt[:, cols]), ALU.mult)
                vec.tensor_tensor((E3, E4)[g % 2][:], h4, over_features(Dt[:, cols]), ALU.mult).then_inc(prod_ready, 1)

            def stage_t(n, g):
                wait(dve, above_ready, n * NG + g + 1)
                wait(dve, t2_done, n * NG + g)
                vec.tensor_tensor(words(T0[:]), words(V[:, g, :]), words(above[:, g % 2, :]), ALU.bitwise_and)
                wait(dve, main_done, n * NG + g + 1 - RT)
                vec.tensor_tensor(words(T1[:, g % RT, :]), words(U[:, g, :]), words(above[:, g % 2, :]),
                                  ALU.bitwise_and).then_inc(t1_done, 1)

            def upper_chunks(n, g):
                if g == 0:
                    wait(dve, s_loaded, 16 * (n + 1))
                wait(dve, masks_ready, n * NG + g - 1)
                for c in range(DVE_CHUNKS):
                    last = vec.tensor_scalar(upper[:, g % 2, c * BI:(c + 1) * BI], s_row[:],
                                             dneg[:, g * CH + c:g * CH + c + 1], ONE, ALU.is_gt, ALU.mult)
                last.then_inc(upper_dve, 1)

            def valid_masks(n, g):
                for half in range(2):
                    u = 2 * g + half
                    wait(dve, adj_loaded[u % NADJ], 16 * (n * (2 * NG // NADJ) + u // NADJ + 1))
                    vec.tensor_scalar(V[:, g, half * HALF:(half + 1) * HALF], adj[:, u % NADJ, :], 0.0, ONE,
                                      ALU.is_gt, ALU.mult).then_inc(adj_used, 1)

            def upper_masks(n, g):
                wait(dve, upper_ready, n * NG + g + 1)
                wait(dve, upper_dve, n * NG + g + 1)
                wait(dve, adj_used, 2 * (n * NG + g + 1))
                vec.tensor_tensor(words(U[:, g, :]), words(V[:, g, :]), words(upper[:, g % 2, :]),
                                  ALU.bitwise_and).then_inc(masks_ready, 1)

            def stage_t2(n, g):
                vec.tensor_tensor(words(T2[:, g % RT, :]), words(T0[:]), words(T1[:, g % RT, :]),
                                  ALU.bitwise_xor).then_inc(t2_done, 1)

            def row_statistics(n):
                count = [0]

                def after(ins):
                    ins.then_inc(dve_step, 1)
                    count[0] += 1
                    wait(dve, dve_step, n * ROW_STEPS + count[0])

                r = [small[:, k, :] for k in range(12)]
                wait(dve, rows_ready, n + 1)
                vec.tensor_tensor(r[0], row_ps[:, :, 0], rows(At, n), ALU.mult)
                vec.tensor_copy(r[7], row_ps[:, :, 2])
                after(vec.tensor_tensor(r[1], row_ps[:, :, 1], rows(Ct, n), ALU.mult))
                after(vec.tensor_tensor(r[2], r[0], r[1], ALU.add))
                after(vec.tensor_scalar(r[3], r[2], TINY, None, ALU.max))
                vec.tensor_scalar(r[5].bitcast(i32), r[3].bitcast(i32), 0x007FFFFF, 0x3F800000,
                                  ALU.bitwise_and, ALU.bitwise_or).then_inc(mant_ready, 1)
                vec.reciprocal(r[8], r[3])
                after(vec.tensor_scalar(r[4].bitcast(i32), r[3].bitcast(i32), 23, None, ALU.logical_shift_right))
                vec.tensor_tensor(r[8], r[8], r[7], ALU.mult)
                after(vec.tensor_scalar(r[4], r[4].bitcast(i32), -127.0, LN2, ALU.add, ALU.mult))
                vec.tensor_tensor(rows(FA, n), r[8], rows(At, n), ALU.mult)
                after(vec.tensor_tensor(r[4], r[4], rows(mthr, n), ALU.add))
                vec.tensor_tensor(rows(FC, n), r[8], rows(Ct, n), ALU.mult).then_inc(factors_ready, 1)
                wait(dve, ln_ready, n + 1)
                after(vec.tensor_tensor(r[9], r[4], r[6], ALU.add))
                after(vec.scalar_tensor_tensor(r[10], r[9], 1.0 / SLOPE, r[9], ALU.mult, ALU.min))
                after(vec.tensor_tensor(r[11], r[10], sdz[:, ds(n * TB, TB), 0], ALU.subtract))
                vec.tensor_tensor(diag[:], id_sb[:].unsqueeze(1).to_broadcast([P, TB, P]),
                                  r[11].unsqueeze(2).to_broadcast([P, TB, P]), ALU.mult).then_inc(diag_ready, 1)
                assert count[0] == ROW_STEPS

            def scale_rows(k):
                wait(dve, tr_done, k + 1)
                wait(dve, factors_ready, k + 1)
                vec.tensor_tensor(E2[:], trC[:].rearrange("p (t f) -> p t f", f=F), over_features(rows(FC, k)),
                                  ALU.mult)
                vec.tensor_tensor(E1[:], trA[:].rearrange("p (t f) -> p t f", f=F), over_features(rows(FA, k)),
                                  ALU.mult).then_inc(scaled, 1)
                wait(dve, scaled, k + 1)
                vec.tensor_tensor(E3[:], E1[:], hh[:].rearrange("p (t f) -> p t f", f=F),
                                  ALU.add).then_inc(y_parts, 1)

            def elu(k):
                wait(dve, ex_ready, k + 1)
                vec.scalar_tensor_tensor(E1[:], E1[:], 0.0, E3[:], ALU.max, ALU.add).then_inc(r_ready, 1)

            def norm_stats(k):
                wait(dve, r2_ready, k + 1)
                for t in range(TB):
                    vec.bn_stats(bn[:, t, :], E1[:, t, :]).then_inc(bn_part, 1)
                for t in range(TB):
                    wait(dve, bn_part, k * TB + t + 1)
                    hold(dve)
                    last = vec.bn_aggr(mv[:, t, :], bn[:, t, :])
                last.then_inc(bn_ready, 1)

            def normalise(k):
                wait(dve, rstd_ready, k + 1)
                wait(dve, out_stored, 16 * (k + 1))
                for t in range(TB):
                    last = vec.tensor_scalar(E4[:, t, :], E1[:, t, :], mv[:, t, 0:1], rstd[:, t:t + 1],
                                             ALU.subtract, ALU.mult)
                last.then_inc(out_ready, 1)

            def step(n, first=False, last=False):
                for g in range(NG):
                    stage_t(n, g)
                    if not last:
                        upper_chunks(n + 1, g)
                    wait(dve, t1_done, n * NG + g + 1)
                    if not last:
                        valid_masks(n + 1, g)
                    stage_t2(n, g)
                    if not last:
                        upper_masks(n + 1, g)
                    if not first and g in stage_e:
                        stage_e[g](n - 1)
                if not last:
                    row_statistics(n + 1)

            stage_e = {1: scale_rows, 3: elu, 5: norm_stats, 7: normalise}
            for g in range(NG):
                upper_chunks(0, g)
                valid_masks(0, g)
                products(g)
                upper_masks(0, g)
            row_statistics(0)
            step(0, first=True)
            with dve.Fori(1, NB - 1) as n:
                step(n)
            step(NB - 1, last=True)
            for g in sorted(stage_e):
                stage_e[g](NB - 1)

        @block.gpsimd
        def _(pool):
            gp = nc.gpsimd
            gp.memset(a_sb[:, 2:3], 1.0)
            gp.memset(ones[:], 1.0)
            gp.memset(minus_half[:], -0.5)
            gp.memset(WV[:], 0.0)
            gp.memset(WU[:], 0.0).then_inc(setup_done, 1)
            pool.wait_ge(top_ready, 1)
            gp.partition_all_reduce(dmax[:], dtop[:], P, bass.bass_isa.ReduceOp.max).then_inc(max_ready, 1)
            for g in range(NG):
                pool.wait_ge(hi_ready, g + 1)
                for dst, src in ((WB, (E1, E2)[g % 2]), (WD, (E3, E4)[g % 2])):
                    last = gp.tensor_tensor(dst[:, g * CH:(g + 1) * CH, 1, :], src[:],
                                            dst[:, g * CH:(g + 1) * CH, 0, :], ALU.subtract)
                last.then_inc(lo_ready, 1)

            def stage_e(k):
                wait(pool, xb_loaded, 32 * (k + 1))
                hold(pool)
                gp.tensor_scalar(xN[:], xN[:], 1.0, None, ALU.subtract).then_inc(xm_done, 1)
                wait(pool, y_parts, k + 1)
                gp.tensor_tensor(E1[:], E3[:], E2[:], ALU.add).then_inc(ysum, 1)
                wait(pool, ysum, k + 1)
                hold(pool)
                gp.tensor_scalar(E2[:], E1[:], 0.0, None, ALU.min).then_inc(y_ready, 1)
                wait(pool, xm_done, k + 1)
                wait(pool, r_ready, k + 1)
                gp.tensor_tensor(E1[:], E1[:], xN[:], ALU.add).then_inc(r2_ready, 1)
                wait(pool, bn_ready, k + 1)
                hold(pool)
                gp.tensor_scalar(vareps[:], mv[:, :, 1], EPS, None, ALU.add).then_inc(ve_ready, 1)
                wait(pool, ve_ready, k + 1)
                gp.tensor_tensor(rstd[:], vareps[:], minus_half[:], ALU.pow).then_inc(rstd_ready, 1)

            stage_e(0)
            with pool.Fori(1, NB) as k:
                stage_e(k)


def kernel(x, adj, L0_gnn_W, L0_gnn_a):
    import concourse.bacc as bacc
    from concourse.bass_utils import run_bass_kernel_spmd

    x, adj, W, a = (np.ascontiguousarray(v) for v in (x, adj, L0_gnn_W, L0_gnn_a))
    part = np.zeros((P, 3), np.float32)
    for q in range(P // SM):
        for row, col in ((0, 0), (1, 0), (2, 0), (3, 1), (4, 1), (5, 1), (6, 2)):
            part[q * SM + row, col] = 1.0
    arrays = {
        "x": x,
        "xT": np.ascontiguousarray(x.T),
        "W": W,
        "WT": np.ascontiguousarray(W.T),
        "a_cols": np.ascontiguousarray(a.reshape(2, F).T),
        "adjT": np.ascontiguousarray(
            adj.reshape(NB, BI, NG, 2, CH // 2, P).transpose(0, 2, 5, 3, 4, 1)).reshape(NB, NG, P, 2, HALF),
        "ident": np.eye(P, dtype=np.float32),
        "sel": part,
    }
    nc = bacc.Bacc("TRN2", target_bir_lowering=False, num_devices=1)
    ins = [nc.dram_tensor(n, v.shape, mybir.dt.from_np(v.dtype), kind="ExternalInput").ap() for n, v in arrays.items()]
    out = nc.dram_tensor("out", (N, F), mybir.dt.float32, kind="ExternalOutput").ap()
    graph_attention(nc, *ins, out)
    return run_bass_kernel_spmd(nc, [arrays], core_ids=[0]).results[0]["out"]
```

```python
from contextlib import ExitStack

import numpy as np
import concourse.bass as bass
from concourse import mybir

P = 128
N = 8192
F = 128
BI = 512
NB = N // BI
TB = BI // P
CH = 4
NG = N // (P * CH)
NC = N // P
GW = CH * BI
HALF = GW // 2
NADJ = 4
RT = 4
NV = 4
LEAD = 8
DVE_CHUNKS = (1, 2, 1, 2)
AT_COPY_ACC = 0
AT_EXP = 5
AT_SCALE, AT_ELU, AT_NORM, AT_OUT = 2, 5, 7, 9
AT_COPY_SUMS = NG - LEAD + 1
AT_SUMS_ROWS = NG - LEAD + 1
AT_ROWS_1 = NG - LEAD + 3
AT_LOG = NG - LEAD + 5
AT_ROWS_2 = NG - LEAD + 6
NXP = 4
XP = N // NXP

THR = 1e-4
SLOPE = 0.2
EPS = 1e-5
SHIFT = 32.0
BIG = float(2 ** 60)
VALID = 0x18
UPPER = 0x08
LOWER = 0x10
V_UNIT, U_UNIT, L_UNIT = 2.0 ** 4, 2.0 ** 6, 2.0 ** 5
WORD = 0x01010101
TINY = 1e-37
LN2 = float(np.log(2.0))
LNTHR = float(np.log(THR))
SM = 32
ROW_STEPS = 9


def graph_attention(nc, x, xT, W, WT, a_cols, adjT, ident, sel, out):
    fp32, bf16, u8, u32, i32 = (mybir.dt.float32, mybir.dt.bfloat16, mybir.dt.uint8, mybir.dt.uint32,
                                mybir.dt.int32)
    fp8 = mybir.dt.float8e4
    ALU = mybir.AluOpType
    ACT = mybir.ActivationFunctionType
    AX = mybir.AxisListType
    ds = bass.ds

    s_dram = nc.dram_tensor("s_rows", (NB, 1, BI), fp32).ap()
    x_blocks = x.rearrange("(n t p) f -> n p t f", t=TB, p=P)
    out_blocks = out.rearrange("(n t p) f -> n p t f", t=TB, p=P)
    xT_blocks = xT.rearrange("f (n i) -> n f i", i=BI)

    with ExitStack() as ctx:
        def sb(name, shape, dt):
            return ctx.enter_context(nc.sbuf_tensor(name, shape, dt))

        def ps(name):
            return ctx.enter_context(nc.psum_tensor(name, [P, BI], fp32))

        def sem(name):
            return ctx.enter_context(nc.semaphore(name))

        V = sb("V", [P, NV, GW], u8)
        C = sb("C", [P, 2, NG, GW], u8)
        adj = sb("adj", [P, NADJ, HALF], i32)
        upper = sb("upper", [P, 2, GW], u8)
        above = sb("above", [P, 2, GW], u8)
        T1 = sb("T1", [P, RT, GW], u8)
        T2 = sb("T2", [P, RT, GW], u8)
        WB = sb("WB", [P, NC, 2, F], bf16)
        WD = sb("WD", [P, NC, 2, F], bf16)
        xT_all = WD[:].rearrange("p c t f -> p (c t f)").bitcast(fp32)
        WV = sb("WV", [P, NC, SM], bf16)
        WC = sb("WC", [P, NC, SM], bf16)
        s_row = sb("s_row", [P, 2, BI], fp32)
        E1 = sb("E1", [P, TB, F], fp32)
        E2 = sb("E2", [P, TB, F], fp32)
        E3 = sb("E3", [P, TB, F], fp32)
        xN = sb("xN", [P, TB, F], fp32)
        accS = [E[:].rearrange("p t f -> p (t f)") for E in (E1, E3)]
        stat_sb = E2[:].rearrange("p t f -> p (t f)")
        diag = E3
        xTb = sb("xTb", [P, BI], fp32)
        W_sb = sb("W_sb", [P, F], fp32)
        WT_sb = sb("WT_sb", [P, F], fp32)
        a_sb = sb("a_sb", [P, 3], fp32)
        wa_sb = sb("wa_sb", [P, 3], fp32)
        id_sb = sb("id_sb", [P, P], fp32)
        ones = sb("ones", [P, P], fp32)
        sel_sb = sb("sel_sb", [P, 3], fp32)
        sdz = sb("sdz", [P, NC, 3], fp32)
        valid = sb("valid", [P, NC], fp32)
        dmask = sb("dmask", [P, NC], fp32)
        dtop = sb("dtop", [P, 1], fp32)
        dmax = sb("dmax", [P, 1], fp32)
        dneg = sb("dneg", [P, NC], fp32)
        dbig = sb("dbig", [P, NC], fp32)
        sc = sb("sc", [P, NC], fp32)
        argB, argA, argC = (E1[:, 0, k * NC:(k + 1) * NC] if k < 2 else E1[:, 1, 0:NC] for k in range(3))
        mrow = sb("mrow", [P, NC], fp32)
        mthr = sb("mthr", [P, NC], fp32)
        At = sb("At", [P, NC], fp32)
        Bt = sb("Bt", [P, NC], fp32)
        Ct = sb("Ct", [P, NC], fp32)
        Dt = sb("Dt", [P, NC], fp32)
        rest = sb("rest", [P, 2, NC], fp32)
        FA = sb("FA", [P, NC], fp32)
        FC = sb("FC", [P, NC], fp32)
        sT = sb("sT", [NC, P], fp32)
        small = sb("small", [P, 12, TB], fp32)
        bn = sb("bn", [P, TB, 6], fp32)
        mv = sb("mv", [P, TB, 2], fp32)
        vareps = sb("vareps", [P, TB], fp32)
        rstd = sb("rstd", [P, TB], fp32)
        minus_half = sb("minus_half", [P, TB], fp32)

        accA, accC, stat, misc, thr, trA, trC, hh = [
            ps(x) for x in ("accA", "accC", "stat", "misc", "thr", "trA", "trC", "hh")]
        sdz_ps = misc[:, 0:3 * NC].rearrange("p (c q) -> p c q", q=3)
        row_ps = misc[:, 192:192 + 3 * TB].rearrange("p (t q) -> p t q", q=3)
        wa_ps = misc[:, 208:211]
        sT_ps = misc[0:NC, 256:256 + P]

        consts_loaded = sem("consts_loaded")
        xT_loaded = [sem(f"xT_loaded{k}") for k in range(NXP)]
        adj_loaded = [sem(f"adj_loaded{k}") for k in range(NADJ)]
        s_loaded = sem("s_loaded")
        xb_loaded = sem("xb_loaded")
        s_stored = sem("s_stored")
        out_stored = sem("out_stored")
        passed = sem("passed")
        setup_done = sem("setup_done")
        wa_ready = sem("wa_ready")
        wa_copied = sem("wa_copied")
        sdz_ready = sem("sdz_ready")
        h_ready = sem("h_ready")
        top_ready = sem("top_ready")
        max_ready = sem("max_ready")
        tab_step = sem("tab_step")
        args_ready = sem("args_ready")
        exps_ready = sem("exps_ready")
        sT_ready = sem("sT_ready")
        sT_copied = sem("sT_copied")
        dbig_ready = sem("dbig_ready")
        stat_weights = sem("stat_weights")
        prod_ready = sem("prod_ready")
        hi_ready = sem("hi_ready")
        lo_ready = sem("lo_ready")
        adj_used = sem("adj_used")
        upper_ready = sem("upper_ready")
        upper_dve = sem("upper_dve")
        masks_ready = sem("masks_ready")
        sums_taken = sem("sums_taken")
        stat_copied = sem("stat_copied")
        rows_ready = sem("rows_ready")
        dve_step = sem("dve_step")
        mant_ready = sem("mant_ready")
        ln_ready = sem("ln_ready")
        diag_ready = sem("diag_ready")
        thr_ready = sem("thr_ready")
        above_ready = sem("above_ready")
        t_done = sem("t_done")
        main_done = sem("main_done")
        acc_copied = sem("acc_copied")
        tr_done = sem("tr_done")
        scaled = sem("scaled")
        y_parts = sem("y_parts")
        xm_done = sem("xm_done")
        ysum = sem("ysum")
        y_ready = sem("y_ready")
        ex_ready = sem("ex_ready")
        r_ready = sem("r_ready")
        r2_ready = sem("r2_ready")
        bn_part = sem("bn_part")
        bn_ready = sem("bn_ready")
        ve_ready = sem("ve_ready")
        rstd_ready = sem("rstd_ready")
        out_ready = sem("out_ready")

        def words(ap):
            return ap.bitcast(u32)

        def wait(eng, semaphore, value):
            if not isinstance(value, int) or value > 0:
                eng.wait_ge(semaphore, value)

        def hold(eng):
            eng.sem_inc(passed, 1)

        def exists(n):
            return not isinstance(n, int) or 0 <= n < NB

        def all_steps(eng, step):
            step(0, 0)
            with eng.Fori(1, NB - 3, 2) as n:
                step(n, 1)
                step(n + 1, 0)
            for n in range(NB - 3, NB):
                step(n, n % 2)

        def rows(tab, n):
            return tab[:, ds(n * TB, TB)]

        def over_features(col):
            return col.unsqueeze(2).to_broadcast([P, TB, F])

        block = ctx.enter_context(nc.Block())

        @block.sync
        def _(sp):
            for dst, src in ((W_sb, W), (WT_sb, WT), (a_sb[:, 0:2], a_cols), (id_sb, ident), (sel_sb, sel)):
                sp.dma_start(dst[:] if dst is not a_sb else dst, src).then_inc(consts_loaded, 16)
            for q in range(NXP):
                sp.dma_start(xT_all[:, q * XP:(q + 1) * XP], xT[:, q * XP:(q + 1) * XP]).then_inc(xT_loaded[q], 16)

            def load_adj(n, g):
                for half in range(2):
                    u = 2 * g + half
                    wait(sp, adj_used, n * 2 * NG + u - NADJ + 1)
                    hold(sp)
                    sp.dma_start(adj[:, u % NADJ, :], adjT[n, g, :, half, :]).then_inc(adj_loaded[u % NADJ], 16)

            def load_s(n, par):
                wait(sp, upper_ready, (n - 1) * NG)
                wait(sp, masks_ready, (n - 1) * NG)
                hold(sp)
                sp.dma_start(s_row[:, par, :], s_dram[n].to_broadcast([P, BI])).then_inc(s_loaded, 16)

            def step(n, par):
                for g in range(NG):
                    ahead = n + 1 + (g + LEAD) // NG
                    if exists(ahead):
                        load_adj(ahead, (g + LEAD) % NG)
                    if g == 1 and exists(n + 2):
                        load_s(n + 2, par)
                    if g == NG - 2:
                        if exists(n - 1):
                            wait(sp, out_ready, n)
                            hold(sp)
                            sp.dma_start(out_blocks[n - 1], xN[:]).then_inc(out_stored, 16)
                            wait(sp, tr_done, n)
                            hold(sp)
                            wait(sp, out_stored, 16 * n)
                            hold(sp)
                        sp.dma_start(xN[:], x_blocks[n]).then_inc(xb_loaded, 16)
                        sp.dma_start(xTb[:], xT_blocks[n]).then_inc(xb_loaded, 16)

            for g in range(NADJ // 2):
                load_adj(0, g)
            sp.wait_ge(sT_copied, 1)
            sp.dma_start(s_dram.rearrange("n o (t p) -> (n o t) p", p=P), sT[:]).then_inc(s_stored, 16)
            sp.wait_ge(s_stored, 16)
            load_s(0, 0)
            sp.wait_ge(s_loaded, 16)
            load_s(1, 1)
            for p in range(NADJ // 2, NG + LEAD):
                load_adj(p // NG, p % NG)
            all_steps(sp, step)
            sp.wait_ge(out_ready, NB)
            sp.dma_start(out_blocks[NB - 1], xN[:]).then_inc(out_stored, 16)
            sp.wait_ge(out_stored, 16 * NB)

        @block.tensor
        def _(pe):
            pe.wait_ge(consts_loaded, 5 * 16)
            pe.wait_ge(setup_done, 1)
            nc.tensor.matmul(wa_ps, WT_sb[:], a_sb[:], start=True, stop=True).then_inc(wa_ready, 1)
            pe.wait_ge(wa_copied, 1)
            for q in range(NXP):
                pe.wait_ge(xT_loaded[q], 16)
                for c in range(q * NC // NXP, (q + 1) * NC // NXP):
                    last = nc.tensor.matmul(sdz_ps[:, c, :], xT_all[:, c * P:(c + 1) * P], wa_sb[:],
                                            start=True, stop=True)
            last.then_inc(sdz_ready, 1)

            def group_h(g):
                wait(pe, prod_ready, g - 1)
                for c in range(CH):
                    k = g * CH + c
                    last = nc.tensor.matmul((trA, trC)[g % 2][:, c * F:(c + 1) * F], xT_all[:, k * P:(k + 1) * P],
                                            W_sb[:], start=True, stop=True)
                last.then_inc(h_ready, 1)

            group_h(0)
            group_h(1)
            pe.wait_ge(tab_step, 1)
            nc.tensor.transpose(sT_ps, sdz[:, :, 0], id_sb[:]).then_inc(sT_ready, 1)

            def stats(n, par, g):
                if g == 0:
                    wait(pe, stat_copied, n)
                wait(pe, masks_ready, n * NG + g + 1)
                hold(pe)
                for masks, weights in ((V[:, g % NV, :], WV), (C[:, par, g, :], WC)):
                    for c in range(CH):
                        last = nc.tensor.matmul(stat[c * SM:(c + 1) * SM, :], weights[:, g * CH + c, :],
                                                masks[:, c * BI:(c + 1) * BI].bitcast(fp8),
                                                start=(g == 0 and weights is WV),
                                                stop=(g == NG - 1 and weights is WC),
                                                tile_position=(0, c * SM))
                last.then_inc(sums_taken, 1)

            def sums_to_rows(n):
                wait(pe, stat_copied, n + 1)
                hold(pe)
                for t in range(TB):
                    last = nc.tensor.matmul(row_ps[:, t, :], stat_sb[:, t * P:(t + 1) * P], sel_sb[:],
                                            start=True, stop=True)
                last.then_inc(rows_ready, 1)

            def threshold(n):
                wait(pe, diag_ready, n + 1)
                wait(pe, above_ready, n * NG)
                hold(pe)
                nc.tensor.matmul(thr[:], ones[:], diag[:].rearrange("p t i -> p (t i)"),
                                 start=True, stop=True).then_inc(thr_ready, 1)

            def main(n, g):
                if g == 0:
                    wait(pe, acc_copied, 2 * n)
                pe.wait_ge(lo_ready, g + 1)
                wait(pe, t_done, n * NG + g + 1)
                hold(pe)
                for acc, masks, weights in ((accA, T1, WB), (accC, T2, WD)):
                    for c in range(CH):
                        for part in range(2):
                            last = nc.tensor.matmul(
                                acc[:], weights[:, g * CH + c, part, :],
                                masks[:, g % RT, c * BI:(c + 1) * BI].bitcast(fp8),
                                start=(g == 0 and c == 0 and part == 0),
                                stop=(g == NG - 1 and c == CH - 1 and part == 1))
                last.then_inc(main_done, 1)

            def to_rows(k):
                wait(pe, acc_copied, 2 * (k + 1))
                wait(pe, xb_loaded, 32 * (k + 1))
                hold(pe)
                for t in range(TB):
                    tile = slice(t * P, (t + 1) * P)
                    nc.tensor.transpose(trA[:, tile], accS[0][:, tile], id_sb[:])
                    nc.tensor.transpose(trC[:, tile], accS[1][:, tile], id_sb[:])
                    last = nc.tensor.matmul(hh[:, tile], xTb[:, tile], W_sb[:], start=True, stop=True)
                last.then_inc(tr_done, 1)

            def step(n, par):
                for g in range(NG):
                    if g == NG - 1 and exists(n + 1):
                        threshold(n + 1)
                    if exists(n):
                        main(n, g)
                    ahead, gg = n + 1 + (g + LEAD) // NG, (g + LEAD) % NG
                    if not exists(n) and g + LEAD + 2 < NG:
                        group_h(g + LEAD + 2)
                    if exists(ahead):
                        stats(ahead, (par + (1 if g + LEAD < NG else 0)) % 2, gg)
                    if g == 0 and exists(n - 1):
                        to_rows(n - 1)
                    if g == AT_SUMS_ROWS and exists(n + 1):
                        sums_to_rows(n + 1)

            pe.wait_ge(stat_weights, 1)
            for g in range(LEAD):
                group_h(g + 2)
                stats(0, 0, g)
            step(-1, 1)
            all_steps(pe, step)
            to_rows(NB - 1)

        @block.scalar
        def _(act):
            act.preload_act_table_set("natural_log_exp_and_others")
            act.wait_ge(sT_ready, 1)
            nc.scalar.copy(sT[:], sT_ps).then_inc(sT_copied, 1)
            act.wait_ge(args_ready, 1)
            nc.scalar.activation(Bt[:], argB, ACT.Exp)
            nc.scalar.activation(Dt[:], argB, ACT.Exp, scale=SLOPE)
            nc.scalar.activation(At[:], argA, ACT.Exp)
            nc.scalar.activation(Ct[:], argC, ACT.Exp).then_inc(exps_ready, 1)

            def test_upper(n, par, g):
                if g == 0:
                    wait(act, s_loaded, 16 * (n + 1))
                wait(act, masks_ready, n * NG + g - 1)
                hold(act)
                for c in range(DVE_CHUNKS[g % 4], CH):
                    last = nc.scalar.activation(upper[:, g % 2, c * BI:(c + 1) * BI].bitcast(fp8),
                                                s_row[:, par, :], ACT.Relu, scale=BIG,
                                                bias=dbig[:, g * CH + c:g * CH + c + 1], saturate=False)
                last.then_inc(upper_ready, 1)

            def test_above(n, g):
                if g == 0:
                    wait(act, thr_ready, n + 1)
                wait(act, t_done, n * NG + g - 1)
                hold(act)
                for c in range(CH):
                    last = nc.scalar.activation(above[:, g % 2, c * BI:(c + 1) * BI].bitcast(fp8), thr[:],
                                                ACT.Relu, scale=-BIG, bias=dbig[:, g * CH + c:g * CH + c + 1],
                                                saturate=False)
                last.then_inc(above_ready, 1)

            def high_parts(g):
                act.wait_ge(prod_ready, g + 1)
                for dst, src in ((WB, (E1, E2)[g % 2]), (WD, (E3, xN)[g % 2])):
                    last = nc.scalar.copy(dst[:, g * CH:(g + 1) * CH, 0, :], src[:])
                last.then_inc(hi_ready, 1)

            def copy_sums(n):
                act.wait_ge(lo_ready, NG)
                wait(act, sums_taken, (n + 1) * NG)
                nc.scalar.copy(stat_sb, stat[:]).then_inc(stat_copied, 1)

            def log_mantissa(n):
                wait(act, mant_ready, n + 1)
                nc.scalar.activation(small[:, 6, :], small[:, 5, :], ACT.Ln).then_inc(ln_ready, 1)

            def copy_acc(n):
                wait(act, main_done, (n + 1) * NG)
                for side, acc in enumerate((accA, accC)):
                    wait(act, tr_done, n)
                    nc.scalar.copy(accS[side], acc[:]).then_inc(acc_copied, 1)

            def exp_negative(k):
                wait(act, y_ready, k + 1)
                nc.scalar.activation(E3[:], E2[:], ACT.Exp).then_inc(ex_ready, 1)

            def step(n, par):
                for g in range(NG):
                    if g == AT_COPY_SUMS and exists(n + 1):
                        copy_sums(n + 1)
                    if exists(n):
                        test_above(n, g)
                    q = g + LEAD + 1
                    if exists(n + 1 + q // NG):
                        test_upper(n + 1 + q // NG, (par + 1 + q // NG) % 2, q % NG)
                    if not exists(n) and q - 1 < NG:
                        high_parts(q - 1)
                    if g == AT_COPY_ACC and exists(n - 1):
                        copy_acc(n - 1)
                    if g == AT_LOG and exists(n + 1):
                        log_mantissa(n + 1)
                    if g == AT_EXP and exists(n - 1):
                        exp_negative(n - 1)

            act.wait_ge(dbig_ready, 1)
            test_upper(0, 0, 0)
            for g in range(LEAD):
                test_upper(0, 0, g + 1)
                high_parts(g)
            step(-1, 1)
            all_steps(act, step)
            copy_acc(NB - 1)
            exp_negative(NB - 1)

        @block.vector
        def _(dve):
            vec = nc.vector
            dve.wait_ge(wa_ready, 1)
            vec.tensor_copy(wa_sb[:], wa_ps).then_inc(wa_copied, 1)
            dve.wait_ge(sdz_ready, 1)
            done = [0]

            def after(ins):
                ins.then_inc(tab_step, 1)
                done[0] += 1
                dve.wait_ge(tab_step, done[0])

            after(vec.tensor_copy(sdz[:], sdz_ps))
            s_tab, d_tab = sdz[:, :, 0], sdz[:, :, 1]
            vec.tensor_scalar(dneg[:], d_tab, -1.0, None, ALU.mult)
            vec.tensor_scalar(dbig[:], d_tab, BIG, None, ALU.mult).then_inc(dbig_ready, 1)
            after(vec.tensor_scalar(valid[:], sdz[:, :, 2], 0.0, None, ALU.not_equal))
            after(vec.tensor_scalar(rest[:, 0, :], valid[:], 1.0, 1e30, ALU.subtract, ALU.mult))
            after(vec.tensor_tensor(dmask[:], rest[:, 0, :], d_tab, ALU.add))
            vec.reduce_max(dtop[:], dmask[:], AX.X).then_inc(top_ready, 1)
            dve.wait_ge(max_ready, 1)
            after(vec.tensor_scalar(argB, d_tab, dmax[:, 0:1], 0.0, ALU.subtract, ALU.min))
            after(vec.tensor_scalar(argB, argB, SHIFT, None, ALU.add))
            after(vec.tensor_scalar(sc[:], s_tab, dmax[:, 0:1], None, ALU.add))
            after(vec.scalar_tensor_tensor(mrow[:], sc[:], SLOPE, sc[:], ALU.mult, ALU.max))
            vec.tensor_scalar(mthr[:], mrow[:], LNTHR, None, ALU.add)
            after(vec.tensor_scalar(sc[:], sc[:], -SHIFT, None, ALU.add))
            vec.tensor_tensor(argA, sc[:], mrow[:], ALU.subtract)
            vec.scalar_tensor_tensor(argC, sc[:], SLOPE, mrow[:], ALU.mult, ALU.subtract).then_inc(args_ready, 1)
            dve.wait_ge(exps_ready, 1)
            vec.tensor_tensor(Bt[:], Bt[:], valid[:], ALU.mult)
            after(vec.tensor_tensor(Dt[:], Dt[:], valid[:], ALU.mult))
            dve.wait_ge(setup_done, 1)
            after(vec.tensor_scalar(WV[:, :, 6], valid[:], V_UNIT, None, ALU.mult))
            for tab, first_col in ((Bt, 0), (Dt, 3)):
                src = tab[:]
                for part in range(3):
                    after(vec.tensor_copy(WC[:, :, first_col + part], src))
                    if part < 2:
                        after(vec.tensor_tensor(rest[:, part, :], src, WC[:, :, first_col + part], ALU.subtract))
                        src = rest[:, part, :]
            vec.tensor_scalar(WV[:, :, 0:3], WC[:, :, 0:3], 2 * V_UNIT, None, ALU.mult)
            after(vec.tensor_scalar(WV[:, :, 3:6], WC[:, :, 3:6], -V_UNIT, None, ALU.mult))
            vec.tensor_scalar(WC[:, :, 0:3], WC[:, :, 0:3], -U_UNIT, None, ALU.mult)
            vec.tensor_scalar(WC[:, :, 3:6], WC[:, :, 3:6], U_UNIT, None, ALU.mult).then_inc(stat_weights, 1)

            def products(g):
                dve.wait_ge(h_ready, g + 1)
                wait(dve, lo_ready, g - 1)
                h4 = (trA, trC)[g % 2][:].rearrange("p (c f) -> p c f", f=F)
                cols = slice(g * CH, (g + 1) * CH)
                vec.tensor_tensor((E1, E2)[g % 2][:], h4, over_features(Bt[:, cols]), ALU.mult)
                vec.tensor_tensor((E3, xN)[g % 2][:], h4, over_features(Dt[:, cols]), ALU.mult).then_inc(prod_ready, 1)

            def stage_t(n, par, g):
                wait(dve, above_ready, n * NG + g + 1)
                wait(dve, main_done, n * NG + g + 1 - RT)
                for T, branch in ((T1, UPPER), (T2, LOWER)):
                    last = vec.scalar_tensor_tensor(words(T[:, g % RT, :]), words(C[:, par, g, :]), branch * WORD,
                                                    words(above[:, g % 2, :]), ALU.bitwise_and, ALU.bitwise_and)
                last.then_inc(t_done, 1)

            def upper_chunks(n, par, g):
                if g == 0:
                    wait(dve, s_loaded, 16 * (n + 1))
                wait(dve, masks_ready, n * NG + g - 1)
                for c in range(DVE_CHUNKS[g % 4]):
                    last = vec.tensor_scalar(upper[:, g % 2, c * BI:(c + 1) * BI], s_row[:, par, :],
                                             dneg[:, g * CH + c:g * CH + c + 1], float(VALID), ALU.is_gt, ALU.mult)
                last.then_inc(upper_dve, 1)

            def valid_masks(n, g):
                wait(dve, sums_taken, n * NG + g + 1 - NV)
                for half in range(2):
                    u = 2 * g + half
                    wait(dve, adj_loaded[u % NADJ], 16 * (n * (2 * NG // NADJ) + u // NADJ + 1))
                    vec.tensor_scalar(V[:, g % NV, half * HALF:(half + 1) * HALF], adj[:, u % NADJ, :], 0.0,
                                      float(VALID), ALU.is_gt, ALU.mult).then_inc(adj_used, 1)

            def branch_masks(n, par, g):
                wait(dve, upper_ready, n * NG + g + 1)
                wait(dve, upper_dve, n * NG + g + 1)
                wait(dve, adj_used, 2 * (n * NG + g + 1))
                vec.scalar_tensor_tensor(words(C[:, par, g, :]), words(upper[:, g % 2, :]), LOWER * WORD,
                                         words(V[:, g % NV, :]), ALU.bitwise_xor, ALU.bitwise_and
                                         ).then_inc(masks_ready, 1)

            r = [small[:, k, :] for k in range(12)]

            def row_factors(n):
                base = n * ROW_STEPS
                wait(dve, rows_ready, n + 1)
                vec.tensor_tensor(r[0], row_ps[:, :, 0], rows(At, n), ALU.mult)
                vec.tensor_copy(r[7], row_ps[:, :, 2])
                vec.tensor_tensor(r[1], row_ps[:, :, 1], rows(Ct, n), ALU.mult).then_inc(dve_step, 1)
                wait(dve, dve_step, base + 1)
                vec.tensor_tensor(r[2], r[0], r[1], ALU.add).then_inc(dve_step, 1)
                wait(dve, dve_step, base + 2)
                vec.tensor_scalar(r[3], r[2], TINY, None, ALU.max).then_inc(dve_step, 1)
                wait(dve, dve_step, base + 3)
                vec.tensor_scalar(r[5].bitcast(i32), r[3].bitcast(i32), 0x007FFFFF, 0x3F800000,
                                  ALU.bitwise_and, ALU.bitwise_or).then_inc(mant_ready, 1)
                vec.reciprocal(r[8], r[3])
                vec.tensor_scalar(r[4].bitcast(i32), r[3].bitcast(i32), 23, None,
                                  ALU.logical_shift_right).then_inc(dve_step, 1)
                wait(dve, dve_step, base + 4)
                vec.tensor_tensor(r[8], r[8], r[7], ALU.mult)
                vec.tensor_scalar(r[4], r[4].bitcast(i32), -127.0, LN2, ALU.add, ALU.mult).then_inc(dve_step, 1)
                wait(dve, dve_step, base + 5)
                vec.scalar_tensor_tensor(rows(FA, n), r[8], U_UNIT, rows(At, n), ALU.mult, ALU.mult)
                vec.scalar_tensor_tensor(rows(FC, n), r[8], L_UNIT, rows(Ct, n), ALU.mult, ALU.mult)
                vec.tensor_tensor(r[4], r[4], rows(mthr, n), ALU.add).then_inc(dve_step, 1)

            def row_thresholds(n):
                base = n * ROW_STEPS
                wait(dve, dve_step, base + 6)
                wait(dve, ln_ready, n + 1)
                vec.tensor_tensor(r[9], r[4], r[6], ALU.add).then_inc(dve_step, 1)
                wait(dve, dve_step, base + 7)
                vec.scalar_tensor_tensor(r[10], r[9], 1.0 / SLOPE, r[9], ALU.mult, ALU.min).then_inc(dve_step, 1)
                wait(dve, dve_step, base + 8)
                vec.tensor_tensor(r[11], r[10], sdz[:, ds(n * TB, TB), 0], ALU.subtract).then_inc(dve_step, 1)
                wait(dve, dve_step, base + 9)
                vec.tensor_tensor(diag[:], id_sb[:].unsqueeze(1).to_broadcast([P, TB, P]),
                                  r[11].unsqueeze(2).to_broadcast([P, TB, P]), ALU.mult).then_inc(diag_ready, 1)

            def scale_rows(k):
                wait(dve, tr_done, k + 1)
                vec.tensor_tensor(E2[:], trC[:].rearrange("p (t f) -> p t f", f=F), over_features(rows(FC, k)),
                                  ALU.mult)
                vec.tensor_tensor(E1[:], trA[:].rearrange("p (t f) -> p t f", f=F), over_features(rows(FA, k)),
                                  ALU.mult).then_inc(scaled, 1)
                wait(dve, scaled, k + 1)
                vec.tensor_tensor(E3[:], E1[:], hh[:].rearrange("p (t f) -> p t f", f=F),
                                  ALU.add).then_inc(y_parts, 1)

            def elu(k):
                wait(dve, ex_ready, k + 1)
                vec.scalar_tensor_tensor(E1[:], E1[:], 0.0, E3[:], ALU.max, ALU.add).then_inc(r_ready, 1)

            def norm_stats(k):
                wait(dve, r2_ready, k + 1)
                for t in range(TB):
                    vec.bn_stats(bn[:, t, :], E1[:, t, :]).then_inc(bn_part, 1)
                for t in range(TB):
                    wait(dve, bn_part, k * TB + t + 1)
                    hold(dve)
                    last = vec.bn_aggr(mv[:, t, :], bn[:, t, :])
                last.then_inc(bn_ready, 1)

            def normalise(k):
                wait(dve, rstd_ready, k + 1)
                for t in range(TB):
                    last = vec.tensor_scalar(xN[:, t, :], E1[:, t, :], mv[:, t, 0:1], rstd[:, t:t + 1],
                                             ALU.subtract, ALU.mult)
                last.then_inc(out_ready, 1)

            stage_e = {AT_SCALE: scale_rows, AT_ELU: elu, AT_NORM: norm_stats, AT_OUT: normalise}

            def step(n, par):
                for g in range(NG):
                    ahead, gg = n + 1 + (g + LEAD) // NG, (g + LEAD) % NG
                    par_ahead = (par + (1 if g + LEAD < NG else 0)) % 2
                    if exists(ahead):
                        valid_masks(ahead, gg)
                        upper_chunks(ahead, par_ahead, gg)
                    if exists(n):
                        stage_t(n, par, g)
                    elif g + LEAD < NG:
                        products(g + LEAD)
                    if exists(ahead):
                        branch_masks(ahead, par_ahead, gg)
                    if g in stage_e and exists(n - 1):
                        stage_e[g](n - 1)
                    if g == AT_ROWS_1 and exists(n + 1):
                        row_factors(n + 1)
                    if g == AT_ROWS_2 and exists(n + 1):
                        row_thresholds(n + 1)

            for g in range(LEAD):
                valid_masks(0, g)
                upper_chunks(0, 0, g)
                products(g)
                branch_masks(0, 0, g)
            step(-1, 1)
            all_steps(dve, step)
            for g in sorted(stage_e):
                stage_e[g](NB - 1)

        @block.gpsimd
        def _(pool):
            gp = nc.gpsimd
            gp.memset(a_sb[:, 2:3], 1.0)
            gp.memset(ones[:], 1.0)
            gp.memset(minus_half[:], -0.5)
            gp.memset(WV[:], 0.0)
            gp.memset(WC[:], 0.0).then_inc(setup_done, 1)
            pool.wait_ge(top_ready, 1)
            gp.partition_all_reduce(dmax[:], dtop[:], P, bass.bass_isa.ReduceOp.max).then_inc(max_ready, 1)
            for g in range(NG):
                pool.wait_ge(hi_ready, g + 1)
                for dst, src in ((WB, (E1, E2)[g % 2]), (WD, (E3, xN)[g % 2])):
                    last = gp.tensor_tensor(dst[:, g * CH:(g + 1) * CH, 1, :], src[:],
                                            dst[:, g * CH:(g + 1) * CH, 0, :], ALU.subtract)
                last.then_inc(lo_ready, 1)

            def stage_e(k):
                wait(pool, xb_loaded, 32 * (k + 1))
                hold(pool)
                gp.tensor_scalar(xN[:], xN[:], 1.0, None, ALU.subtract).then_inc(xm_done, 1)
                wait(pool, y_parts, k + 1)
                gp.tensor_tensor(E1[:], E3[:], E2[:], ALU.add).then_inc(ysum, 1)
                wait(pool, ysum, k + 1)
                hold(pool)
                gp.tensor_scalar(E2[:], E1[:], 0.0, None, ALU.min).then_inc(y_ready, 1)
                wait(pool, xm_done, k + 1)
                wait(pool, r_ready, k + 1)
                gp.tensor_tensor(E1[:], E1[:], xN[:], ALU.add).then_inc(r2_ready, 1)
                wait(pool, bn_ready, k + 1)
                hold(pool)
                gp.tensor_scalar(vareps[:], mv[:, :, 1], EPS, None, ALU.add).then_inc(ve_ready, 1)
                wait(pool, ve_ready, k + 1)
                gp.tensor_tensor(rstd[:], vareps[:], minus_half[:], ALU.pow).then_inc(rstd_ready, 1)

            stage_e(0)
            with pool.Fori(1, NB) as k:
                stage_e(k)


def kernel(x, adj, L0_gnn_W, L0_gnn_a):
    import concourse.bacc as bacc
    from concourse.bass_utils import run_bass_kernel_spmd

    x, adj, W, a = (np.ascontiguousarray(v) for v in (x, adj, L0_gnn_W, L0_gnn_a))
    part = np.zeros((P, 3), np.float32)
    for q in range(P // SM):
        for row, col in ((0, 0), (1, 0), (2, 0), (3, 1), (4, 1), (5, 1), (6, 2)):
            part[q * SM + row, col] = 1.0
    arrays = {
        "x": x,
        "xT": np.ascontiguousarray(x.T),
        "W": W,
        "WT": np.ascontiguousarray(W.T),
        "a_cols": np.ascontiguousarray(a.reshape(2, F).T),
        "adjT": np.ascontiguousarray(
            adj.reshape(NB, BI, NG, 2, CH // 2, P).transpose(0, 2, 5, 3, 4, 1)).reshape(NB, NG, P, 2, HALF),
        "ident": np.eye(P, dtype=np.float32),
        "sel": part,
    }
    nc = bacc.Bacc("TRN2", target_bir_lowering=False, num_devices=1)
    ins = [nc.dram_tensor(n, v.shape, mybir.dt.from_np(v.dtype), kind="ExternalInput").ap() for n, v in arrays.items()]
    out = nc.dram_tensor("out", (N, F), mybir.dt.float32, kind="ExternalOutput").ap()
    graph_attention(nc, *ins, out)
    return run_bass_kernel_spmd(nc, [arrays], core_ids=[0]).results[0]["out"]
```

```python
from contextlib import ExitStack

import numpy as np
import concourse.bass as bass
from concourse import mybir

P = 128
N = 8192
F = 128
BI = 512
NB = N // BI
TB = BI // P
CH = 4
NG = N // (P * CH)
NC = N // P
GW = CH * BI
HALF = GW // 2
NADJ = 4
RT = 4
NV = 4
NA = 4
LEAD = 7
DVE_CHUNKS = 3 * (1, 1, 1, 2) + (1, 2, 1, 2)
DVE_CHUNKS_0 = (0, 1, 0, 1)
EARLY = 3
AT_COPY_ACC = 0
AT_SCALE = 2
AT_EXP = 4
AT_ELU, AT_NORM, AT_OUT = 5, 7, 9
AT_COPY_SUMS = 11
AT_SUMS_ROWS = 10
AT_ROWS_1 = 13
AT_LOG = 14
AT_ROWS_2 = 14
AT_THRESHOLD = 14
NXP = 8
XP = N // NXP
DIRECT = 3
NC_DRAM = NC - DIRECT * XP // P

THR = 1e-4
SLOPE = 0.2
EPS = 1e-5
SHIFT = 32.0
BIG = float(2 ** 60)
VALID = 0x18
UPPER = 0x08
LOWER = 0x10
V_UNIT, U_UNIT, L_UNIT = 2.0 ** 4, 2.0 ** 6, 2.0 ** 5
WORD = 0x01010101
TINY = 1e-37
LN2 = float(np.log(2.0))
LNTHR = float(np.log(THR))
SM = 32
ROW_STEPS = 9


def graph_attention(nc, x, xT, W, WT, a_cols, adjT, ident, out):
    fp32, bf16, u8, u32, i32 = (mybir.dt.float32, mybir.dt.bfloat16, mybir.dt.uint8, mybir.dt.uint32,
                                mybir.dt.int32)
    fp8 = mybir.dt.float8e4
    ALU = mybir.AluOpType
    ACT = mybir.ActivationFunctionType
    AX = mybir.AxisListType
    ds = bass.ds

    sdz_dram = nc.dram_tensor("sdz_rows", (3, N), fp32).ap()
    s_dram = sdz_dram[0:1, :].rearrange("o (n i) -> n o i", i=BI)
    x_blocks = x.rearrange("(n t p) f -> n p t f", t=TB, p=P)
    out_blocks = out.rearrange("(n t p) f -> n p t f", t=TB, p=P)
    xT_blocks = xT.rearrange("f (n i) -> n f i", i=BI)

    with ExitStack() as ctx:
        def sb(name, shape, dt):
            return ctx.enter_context(nc.sbuf_tensor(name, shape, dt))

        def ps(name):
            return ctx.enter_context(nc.psum_tensor(name, [P, BI], fp32))

        def sem(name):
            return ctx.enter_context(nc.semaphore(name))

        V = sb("V", [P, NV, GW], u8)
        C = sb("C", [P, 2, NG, GW], u8)
        adj = sb("adj", [P, NADJ, HALF], i32)
        upper = sb("upper", [P, 2, GW], u8)
        above = sb("above", [P, NA, GW], u8)
        T1 = sb("T1", [P, RT, GW], u8)
        T2 = sb("T2", [P, RT, GW], u8)
        WB = sb("WB", [P, NC, 2, F], bf16)
        WD = sb("WD", [P, NC, 2, F], bf16)
        xT_all = WD[:].rearrange("p c t f -> p (c t f)").bitcast(fp32)
        WV = sb("WV", [P, NC, SM], bf16)
        WC = sb("WC", [P, NC, SM], bf16)
        s_row = sb("s_row", [P, 2, BI], fp32)
        E1 = sb("E1", [P, TB, F], fp32)
        E2 = sb("E2", [P, TB, F], fp32)
        E3 = sb("E3", [P, TB, F], fp32)
        xN = sb("xN", [P, TB, F], fp32)
        accS = [E[:].rearrange("p t f -> p (t f)") for E in (E1, E3)]
        stat_sb = E2[:].rearrange("p t f -> p (t f)")
        xTb = sb("xTb", [P, BI], fp32)
        W_sb = sb("W_sb", [P, F], fp32)
        WT_sb = E3[:, 0, :]
        a_sb = sb("a_sb", [P, 3], fp32)
        wa_sb = sb("wa_sb", [P, 3], fp32)
        id_sb = sb("id_sb", [P, P], fp32)
        sdz_rows = C[0:3, 1, :, :].rearrange("p g m -> p (g m)").bitcast(fp32)
        sdz_chunks = E2[0:NC_DRAM, 0:3, :]
        sdz = sb("sdz", [P, 3, NC], fp32)
        valid, dmask, sc, mrow = (E2[:, 1 + k // 2, k % 2 * NC:(k % 2 + 1) * NC] for k in range(4))
        rest = E2[:, 0, :].rearrange("p (b c) -> p b c", b=2)
        dtop = sb("dtop", [P, 1], fp32)
        dmax = sb("dmax", [P, 1], fp32)
        dneg = sb("dneg", [P, NC], fp32)
        dbig = sb("dbig", [P, NC], fp32)
        argB, argA, argC = E1[:, 0, 0:NC], E1[:, 0, NC:2 * NC], E1[:, 1, 0:NC]
        exp_bias = sb("exp_bias", [P, 4], fp32)
        mthr = sb("mthr", [P, NC], fp32)
        At = sb("At", [P, NC], fp32)
        BD = sb("BD", [P, 2, NC], fp32)
        Bt, Dt = BD[:, 0, :], BD[:, 1, :]
        Ct = sb("Ct", [P, NC], fp32)
        FA = sb("FA", [P, NC], fp32)
        FC = sb("FC", [P, NC], fp32)
        small = sb("small", [P, 12, TB], fp32)
        zl = sb("zl", [P, TB, 3], fp32)
        bn = sb("bn", [P, TB, 6], fp32)
        mv = sb("mv", [P, TB, 2], fp32)
        vareps = sb("vareps", [P, TB], fp32)
        rstd = sb("rstd", [P, TB], fp32)
        minus_half = sb("minus_half", [P, TB], fp32)

        accA, accC, stat, misc, thr, trA, trC, hh = [
            ps(x) for x in ("accA", "accC", "stat", "misc", "thr", "trA", "trC", "hh")]
        sdz_ps = misc[:, 0:3 * NC].rearrange("p (q c) -> p c q", c=NC)
        row_ps = misc[:].rearrange("p (t m) -> p t m", m=P)
        wa_ps = misc[:, 208:211]
        row_banks = [b[0:3, :] for b in (accA, accC, thr, hh)]

        consts_loaded = sem("consts_loaded")
        xT_loaded = [sem(f"xT_loaded{k}") for k in range(NXP)]
        adj_loaded = [sem(f"adj_loaded{k}") for k in range(NADJ)]
        s_loaded = sem("s_loaded")
        xb_loaded = sem("xb_loaded")
        sdz_stored = sem("sdz_stored")
        last_stored = sem("last_stored")
        chunks_loaded = sem("chunks_loaded")
        out_stored = sem("out_stored")
        passed = sem("passed")
        setup_done = sem("setup_done")
        wa_ready = sem("wa_ready")
        wa_copied = sem("wa_copied")
        row_made = sem("row_made")
        row_copied = sem("row_copied")
        sdz_ready = sem("sdz_ready")
        h_ready = sem("h_ready")
        top_ready = sem("top_ready")
        max_ready = sem("max_ready")
        tab_step = sem("tab_step")
        args_ready = sem("args_ready")
        exps_ready = sem("exps_ready")
        dbig_ready = sem("dbig_ready")
        stat_weights = sem("stat_weights")
        prod_ready = sem("prod_ready")
        hi_ready = sem("hi_ready")
        lo_ready = sem("lo_ready")
        adj_used = sem("adj_used")
        upper_ready = sem("upper_ready")
        upper_dve = sem("upper_dve")
        masks_ready = sem("masks_ready")
        sums_taken = sem("sums_taken")
        stat_copied = sem("stat_copied")
        rows_ready = sem("rows_ready")
        zl_ready = sem("zl_ready")
        dve_step = sem("dve_step")
        mant_ready = sem("mant_ready")
        ln_ready = sem("ln_ready")
        thr_ready = sem("thr_ready")
        above_ready = sem("above_ready")
        t_done = sem("t_done")
        main_done = sem("main_done")
        accA_done = sem("accA_done")
        acc_copied = sem("acc_copied")
        trA_done = sem("trA_done")
        tr_done = sem("tr_done")
        scaled = sem("scaled")
        y_parts = sem("y_parts")
        xm_done = sem("xm_done")
        ysum = sem("ysum")
        y_ready = sem("y_ready")
        ex_ready = sem("ex_ready")
        r_ready = sem("r_ready")
        r2_ready = sem("r2_ready")
        bn_part = sem("bn_part")
        bn_ready = sem("bn_ready")
        ve_ready = sem("ve_ready")
        rstd_ready = sem("rstd_ready")
        out_ready = sem("out_ready")

        def words(ap):
            return ap.bitcast(u32)

        def wait(eng, semaphore, value):
            if not isinstance(value, int) or value > 0:
                eng.wait_ge(semaphore, value)

        def hold(eng):
            eng.sem_inc(passed, 1)

        def exists(n):
            return not isinstance(n, int) or 0 <= n < NB

        def dve_chunks(n, g):
            chunks = DVE_CHUNKS_0 if isinstance(n, int) and n == 0 else DVE_CHUNKS
            return chunks[g % len(chunks)]

        def all_steps(eng, step):
            step(0, 0)
            with eng.Fori(1, NB - 3, 2) as n:
                step(n, 1)
                step(n + 1, 0)
            for n in range(NB - 3, NB):
                step(n, n % 2)

        def rows(tab, n):
            return tab[:, ds(n * TB, TB)]

        def over_features(col):
            return col.unsqueeze(2).to_broadcast([P, TB, F])

        block = ctx.enter_context(nc.Block())

        @block.sync
        def _(sp):
            for dst, src in ((W_sb[:], W), (WT_sb, WT), (a_sb[:, 0:2], a_cols), (id_sb[:], ident)):
                sp.dma_start(dst, src).then_inc(consts_loaded, 16)
            for q in range(NXP):
                sp.dma_start(xT_all[:, q * XP:(q + 1) * XP], xT[:, q * XP:(q + 1) * XP]).then_inc(xT_loaded[q], 16)

            def load_adj(n, g):
                for half in range(2):
                    u = 2 * g + half
                    wait(sp, adj_used, n * 2 * NG + u - NADJ + 1)
                    hold(sp)
                    sp.dma_start(adj[:, u % NADJ, :], adjT[n, g, :, half, :]).then_inc(adj_loaded[u % NADJ], 16)

            def load_s(n, par):
                wait(sp, upper_ready, (n - 1) * NG)
                wait(sp, masks_ready, (n - 1) * NG)
                hold(sp)
                sp.dma_start(s_row[:, par, :], s_dram[n].to_broadcast([P, BI])).then_inc(s_loaded, 16)

            def step(n, par):
                for g in range(NG):
                    ahead = n + 1 + (g + LEAD) // NG
                    if exists(ahead):
                        load_adj(ahead, (g + LEAD) % NG)
                    if g == 1 and exists(n + 2):
                        load_s(n + 2, par)
                    if g == NG - 2:
                        if exists(n - 1):
                            wait(sp, out_ready, n)
                            hold(sp)
                            sp.dma_start(out_blocks[n - 1], xN[:]).then_inc(out_stored, 16)
                            wait(sp, tr_done, n)
                            hold(sp)
                            wait(sp, out_stored, 16 * n)
                            hold(sp)
                        sp.dma_start(xN[:], x_blocks[n]).then_inc(xb_loaded, 16)
                        sp.dma_start(xTb[:], xT_blocks[n]).then_inc(xb_loaded, 16)

            for g in range(EARLY):
                load_adj(0, g)
            sp.wait_ge(sdz_stored, 16 * (NXP - DIRECT))
            load_s(0, 0)
            sp.wait_ge(s_loaded, 16)
            load_s(1, 1)
            sp.wait_ge(last_stored, 16 * DIRECT)
            for p in range(EARLY, NG + LEAD):
                load_adj(p // NG, p % NG)
            all_steps(sp, step)
            sp.wait_ge(out_ready, NB)
            sp.dma_start(out_blocks[NB - 1], xN[:]).then_inc(out_stored, 16)
            sp.wait_ge(out_stored, 16 * NB)

        @block.tensor
        def _(pe):
            pe.wait_ge(consts_loaded, 4 * 16)
            pe.wait_ge(setup_done, 1)
            nc.tensor.matmul(wa_ps, WT_sb, a_sb[:], start=True, stop=True).then_inc(wa_ready, 1)
            pe.wait_ge(wa_copied, 1)
            for q in range(NXP):
                pe.wait_ge(xT_loaded[q], 16)
                for b in range(q * NB // NXP, (q + 1) * NB // NXP):
                    wait(pe, row_copied, b + 1 - len(row_banks))
                    nc.tensor.matmul(row_banks[b % len(row_banks)], wa_sb[:], xT_all[:, b * BI:(b + 1) * BI],
                                     start=True, stop=True).then_inc(row_made, 1)

            def group_h(g):
                wait(pe, prod_ready, g - 1)
                for c in range(CH):
                    k = g * CH + c
                    last = nc.tensor.matmul((trA, trC)[g % 2][:, c * F:(c + 1) * F], xT_all[:, k * P:(k + 1) * P],
                                            W_sb[:], start=True, stop=True)
                last.then_inc(h_ready, 1)

            pe.wait_ge(row_copied, NB)
            for c in range(NC_DRAM, NC):
                nc.tensor.transpose(sdz_ps[:, c, :], sdz_rows[:, c * P:(c + 1) * P], id_sb[0:3, 0:3])
            pe.wait_ge(chunks_loaded, 16)
            for q in range(3):
                last = nc.tensor.transpose(sdz_ps[:, 0:NC_DRAM, q], sdz_chunks[:, q, :], id_sb[0:NC_DRAM, 0:NC_DRAM])
            last.then_inc(sdz_ready, 1)
            group_h(0)
            group_h(1)

            def stats(n, par, g):
                if g == 0:
                    wait(pe, stat_copied, n)
                wait(pe, masks_ready, n * NG + g + 1)
                hold(pe)
                for masks, weights in ((V[:, g % NV, :], WV), (C[:, par, g, :], WC)):
                    for c in range(CH):
                        last = nc.tensor.matmul(stat[c * SM:(c + 1) * SM, :], weights[:, g * CH + c, :],
                                                masks[:, c * BI:(c + 1) * BI].bitcast(fp8),
                                                start=(g == 0 and weights is WV),
                                                stop=(g == NG - 1 and weights is WC),
                                                tile_position=(0, c * SM))
                last.then_inc(sums_taken, 1)

            def sums_to_rows(n):
                wait(pe, stat_copied, n + 1)
                hold(pe)
                for t in range(TB):
                    last = nc.tensor.transpose(row_ps[:, t, :], stat_sb[:, t * P:(t + 1) * P], id_sb[:])
                last.then_inc(rows_ready, 1)

            def threshold(n):
                wait(pe, dve_step, (n + 1) * ROW_STEPS)
                wait(pe, above_ready, n * NG)
                hold(pe)
                for t in range(TB):
                    last = nc.tensor.transpose(thr[:, t * P:(t + 1) * P], small[:, 11, t:t + 1].to_broadcast([P, P]),
                                               id_sb[:])
                last.then_inc(thr_ready, 1)

            def main(n, g):
                pe.wait_ge(lo_ready, g + 1)
                wait(pe, t_done, n * NG + g + 1)
                hold(pe)
                for side, (acc, masks, weights) in enumerate(((accA, T1, WB), (accC, T2, WD))):
                    if side == 1 and g == AT_THRESHOLD and exists(n + 1):
                        threshold(n + 1)
                    if g == 0:
                        wait(pe, acc_copied, 2 * n - 1 + side)
                        hold(pe)
                    for c in range(CH):
                        for part in range(2):
                            last = nc.tensor.matmul(
                                acc[:], weights[:, g * CH + c, part, :],
                                masks[:, g % RT, c * BI:(c + 1) * BI].bitcast(fp8),
                                start=(g == 0 and c == 0 and part == 0),
                                stop=(g == NG - 1 and c == CH - 1 and part == 1))
                    if g == NG - 1 and side == 0:
                        last.then_inc(accA_done, 1)
                last.then_inc(main_done, 1)

            def to_rows(k):
                tiles = [slice(t * P, (t + 1) * P) for t in range(TB)]
                wait(pe, xb_loaded, 32 * (k + 1))
                hold(pe)
                for tile in tiles:
                    nc.tensor.matmul(hh[:, tile], xTb[:, tile], W_sb[:], start=True, stop=True)
                wait(pe, acc_copied, 2 * k + 1)
                hold(pe)
                for tile in tiles:
                    last = nc.tensor.transpose(trA[:, tile], accS[0][:, tile], id_sb[:])
                last.then_inc(trA_done, 1)
                wait(pe, acc_copied, 2 * k + 2)
                hold(pe)
                for tile in tiles:
                    last = nc.tensor.transpose(trC[:, tile], accS[1][:, tile], id_sb[:])
                last.then_inc(tr_done, 1)

            def step(n, par):
                for g in range(NG):
                    if exists(n):
                        main(n, g)
                    elif g == AT_THRESHOLD:
                        threshold(n + 1)
                    ahead, gg = n + 1 + (g + LEAD) // NG, (g + LEAD) % NG
                    if not exists(n) and g + LEAD + 2 < NG:
                        group_h(g + LEAD + 2)
                    if exists(ahead):
                        stats(ahead, (par + (1 if g + LEAD < NG else 0)) % 2, gg)
                    if g == 0 and exists(n - 1):
                        to_rows(n - 1)
                    if g == AT_SUMS_ROWS and exists(n + 1):
                        sums_to_rows(n + 1)

            pe.wait_ge(stat_weights, 1)
            for g in range(LEAD):
                group_h(g + 2)
                stats(0, 0, g)
            step(-1, 1)
            all_steps(pe, step)
            to_rows(NB - 1)

        @block.scalar
        def _(act):
            act.preload_act_table_set("natural_log_exp_and_others")
            for b in range(NB):
                act.wait_ge(row_made, b + 1)
                nc.scalar.copy(sdz_rows[:, b * BI:(b + 1) * BI], row_banks[b % len(row_banks)]).then_inc(row_copied, 1)
                if (b + 1) * BI % XP == 0:
                    act.wait_ge(row_copied, b + 1)
                    piece = slice((b + 1) * BI - XP, (b + 1) * BI)
                    act.dma_start(sdz_dram[:, piece], sdz_rows[:, piece]
                                  ).then_inc(sdz_stored if b < NB - DIRECT * XP // BI else last_stored, 16)
                if b == NB - DIRECT:
                    act.wait_ge(sdz_stored, 16 * (NXP - DIRECT))
                    act.dma_start(sdz_chunks, sdz_dram[:, 0:NC_DRAM * P].rearrange("q (c p) -> c q p", p=P)
                                  ).then_inc(chunks_loaded, 16)

            def test_upper(n, par, g):
                if g == 0:
                    wait(act, s_loaded, 16 * (n + 1))
                wait(act, masks_ready, n * NG + g - 1)
                hold(act)
                for c in range(dve_chunks(n, g), CH):
                    last = nc.scalar.activation(upper[:, g % 2, c * BI:(c + 1) * BI].bitcast(fp8),
                                                s_row[:, par, :], ACT.Relu, scale=BIG,
                                                bias=dbig[:, g * CH + c:g * CH + c + 1], saturate=False)
                last.then_inc(upper_ready, 1)

            def test_above(n, g):
                if g == 0:
                    wait(act, thr_ready, n + 1)
                wait(act, t_done, n * NG + g + 1 - NA)
                hold(act)
                for c in range(CH):
                    last = nc.scalar.activation(above[:, g % NA, c * BI:(c + 1) * BI].bitcast(fp8), thr[:],
                                                ACT.Relu, scale=-BIG, bias=dbig[:, g * CH + c:g * CH + c + 1],
                                                saturate=False)
                last.then_inc(above_ready, 1)

            def high_parts(g):
                act.wait_ge(prod_ready, g + 1)
                for dst, src in ((WB, (E1, E2)[g % 2]), (WD, (E3, xN)[g % 2])):
                    last = nc.scalar.copy(dst[:, g * CH:(g + 1) * CH, 0, :], src[:])
                last.then_inc(hi_ready, 1)

            def copy_sums(n):
                act.wait_ge(lo_ready, NG)
                wait(act, sums_taken, (n + 1) * NG)
                nc.scalar.copy(stat_sb, stat[:]).then_inc(stat_copied, 1)

            def log_mantissa(n):
                wait(act, mant_ready, n + 1)
                nc.scalar.activation(small[:, 6, :], small[:, 5, :], ACT.Ln).then_inc(ln_ready, 1)

            def copy_acc(n):
                wait(act, tr_done, n)
                hold(act)
                for side, acc in enumerate((accA, accC)):
                    wait(act, *((accA_done, n + 1), (main_done, (n + 1) * NG))[side])
                    nc.scalar.copy(accS[side], acc[:]).then_inc(acc_copied, 1)

            def exp_negative(k):
                wait(act, y_ready, k + 1)
                nc.scalar.activation(E3[:], E2[:], ACT.Exp).then_inc(ex_ready, 1)

            def step(n, par):
                for g in range(NG):
                    if g == AT_COPY_SUMS and exists(n + 1):
                        copy_sums(n + 1)
                    if exists(n):
                        test_above(n, g)
                    q = g + LEAD + 1
                    if exists(n + 1 + q // NG):
                        test_upper(n + 1 + q // NG, (par + 1 + q // NG) % 2, q % NG)
                    if not exists(n) and q - 1 < NG:
                        high_parts(q - 1)
                    if g == AT_COPY_ACC and exists(n - 1):
                        copy_acc(n - 1)
                    if g == AT_LOG and exists(n + 1):
                        log_mantissa(n + 1)
                    if g == AT_EXP and exists(n - 1):
                        exp_negative(n - 1)

            act.wait_ge(dbig_ready, 1)
            test_upper(0, 0, 0)
            act.wait_ge(args_ready, 1)
            for k, (dst, arg, scale) in enumerate(((Bt, argB, 1.0), (Dt, argB, SLOPE), (At[:], argA, 1.0),
                                                   (Ct[:], argC, 1.0))):
                last = nc.scalar.activation(dst, arg, ACT.Exp, scale=scale, bias=exp_bias[:, k:k + 1])
            last.then_inc(exps_ready, 1)
            for g in range(LEAD):
                test_upper(0, 0, g + 1)
                high_parts(g)
            step(-1, 1)
            all_steps(act, step)
            copy_acc(NB - 1)
            exp_negative(NB - 1)

        @block.vector
        def _(dve):
            vec = nc.vector
            dve.wait_ge(wa_ready, 1)
            vec.tensor_copy(wa_sb[:], wa_ps).then_inc(wa_copied, 1)

            def valid_masks(n, g):
                wait(dve, sums_taken, n * NG + g + 1 - NV)
                for half in range(2):
                    u = 2 * g + half
                    wait(dve, adj_loaded[u % NADJ], 16 * (n * (2 * NG // NADJ) + u // NADJ + 1))
                    vec.tensor_scalar(V[:, g % NV, half * HALF:(half + 1) * HALF], adj[:, u % NADJ, :], 0.0,
                                      float(VALID), ALU.is_gt, ALU.mult).then_inc(adj_used, 1)

            for g in range(EARLY):
                valid_masks(0, g)
            dve.wait_ge(sdz_ready, 1)
            done = [0]

            def after(ins):
                ins.then_inc(tab_step, 1)
                done[0] += 1
                dve.wait_ge(tab_step, done[0])

            after(vec.tensor_copy(sdz[:], misc[:, 0:3 * NC].rearrange("p (q c) -> p q c", q=3)))
            s_tab, d_tab = sdz[:, 0, :], sdz[:, 1, :]
            vec.tensor_scalar(dbig[:], d_tab, BIG, None, ALU.mult).then_inc(dbig_ready, 1)
            after(vec.tensor_scalar(valid, sdz[:, 2, :], 0.0, None, ALU.not_equal))
            after(vec.tensor_scalar(dmask, valid, 1.0, 1e30, ALU.subtract, ALU.mult))
            after(vec.tensor_tensor(dmask, dmask, d_tab, ALU.add))
            vec.reduce_max(dtop[:], dmask, AX.X).then_inc(top_ready, 1)
            vec.tensor_scalar(dneg[:], d_tab, -1.0, None, ALU.mult)
            vec.tensor_scalar(WV[:, :, 6], valid, V_UNIT, None, ALU.mult)
            dve.wait_ge(max_ready, 1)
            after(vec.tensor_scalar(sc, s_tab, dmax[:, 0:1], None, ALU.add))
            vec.tensor_scalar(argB, d_tab, dmax[:, 0:1], 0.0, ALU.subtract, ALU.min)
            after(vec.scalar_tensor_tensor(mrow, sc, SLOPE, sc, ALU.mult, ALU.max))
            vec.tensor_tensor(argA, sc, mrow, ALU.subtract)
            vec.scalar_tensor_tensor(argC, sc, SLOPE, mrow, ALU.mult, ALU.subtract).then_inc(args_ready, 1)
            vec.tensor_scalar(mthr[:], mrow, LNTHR, None, ALU.add)
            dve.wait_ge(exps_ready, 1)
            after(vec.tensor_tensor(BD[:], BD[:], valid.unsqueeze(1).to_broadcast([P, 2, NC]), ALU.mult))
            WC_parts = WC[:, :, 0:6].rearrange("p c (b t) -> p b c t", b=2)
            left = BD[:]
            for part in range(3):
                after(vec.tensor_copy(WC_parts[:, :, :, part], left))
                if part < 2:
                    after(vec.tensor_tensor(rest, left, WC_parts[:, :, :, part], ALU.subtract))
                    left = rest
            vec.tensor_scalar(WV[:, :, 0:3], WC[:, :, 0:3], 2 * V_UNIT, None, ALU.mult)
            after(vec.tensor_scalar(WV[:, :, 3:6], WC[:, :, 3:6], -V_UNIT, None, ALU.mult))
            vec.tensor_scalar(WC[:, :, 0:3], WC[:, :, 0:3], -U_UNIT, None, ALU.mult)
            vec.tensor_scalar(WC[:, :, 3:6], WC[:, :, 3:6], U_UNIT, None, ALU.mult).then_inc(stat_weights, 1)

            def products(g):
                dve.wait_ge(h_ready, g + 1)
                wait(dve, lo_ready, g - 1)
                h4 = (trA, trC)[g % 2][:].rearrange("p (c f) -> p c f", f=F)
                cols = slice(g * CH, (g + 1) * CH)
                vec.tensor_tensor((E1, E2)[g % 2][:], h4, over_features(Bt[:, cols]), ALU.mult)
                vec.tensor_tensor((E3, xN)[g % 2][:], h4, over_features(Dt[:, cols]), ALU.mult).then_inc(prod_ready, 1)

            def stage_t(n, par, g):
                wait(dve, above_ready, n * NG + g + 1)
                wait(dve, main_done, n * NG + g + 1 - RT)
                for T, branch in ((T1, UPPER), (T2, LOWER)):
                    last = vec.scalar_tensor_tensor(words(T[:, g % RT, :]), words(C[:, par, g, :]), branch * WORD,
                                                    words(above[:, g % NA, :]), ALU.bitwise_and, ALU.bitwise_and)
                last.then_inc(t_done, 1)

            def upper_chunks(n, par, g):
                if g == 0:
                    wait(dve, s_loaded, 16 * (n + 1))
                wait(dve, masks_ready, n * NG + g - 1)
                for c in range(dve_chunks(n, g)):
                    last = vec.tensor_scalar(upper[:, g % 2, c * BI:(c + 1) * BI], s_row[:, par, :],
                                             dneg[:, g * CH + c:g * CH + c + 1], float(VALID), ALU.is_gt, ALU.mult)
                if dve_chunks(n, g):
                    last.then_inc(upper_dve, 1)
                else:
                    dve.sem_inc(upper_dve, 1)

            def branch_masks(n, par, g):
                wait(dve, upper_ready, n * NG + g + 1)
                wait(dve, upper_dve, n * NG + g + 1)
                wait(dve, adj_used, 2 * (n * NG + g + 1))
                vec.scalar_tensor_tensor(words(C[:, par, g, :]), words(upper[:, g % 2, :]), LOWER * WORD,
                                         words(V[:, g % NV, :]), ALU.bitwise_xor, ALU.bitwise_and
                                         ).then_inc(masks_ready, 1)

            r = [small[:, k, :] for k in range(12)]

            def row_factors(n):
                base = n * ROW_STEPS
                wait(dve, rows_ready, n + 1)
                vec.tensor_reduce(zl[:], row_ps.rearrange("p t (q m) -> p t q m", m=SM)[:, :, :, 0:9].rearrange(
                    "p t q (k s) -> p t k q s", s=3), AX.XY, ALU.add).then_inc(zl_ready, 1)
                wait(dve, zl_ready, n + 1)
                vec.tensor_tensor(r[0], zl[:, :, 0], rows(At, n), ALU.mult)
                vec.tensor_tensor(r[1], zl[:, :, 1], rows(Ct, n), ALU.mult).then_inc(dve_step, 1)
                wait(dve, dve_step, base + 1)
                vec.tensor_tensor(r[2], r[0], r[1], ALU.add).then_inc(dve_step, 1)
                wait(dve, dve_step, base + 2)
                vec.tensor_scalar(r[3], r[2], TINY, None, ALU.max).then_inc(dve_step, 1)
                wait(dve, dve_step, base + 3)
                vec.tensor_scalar(r[5].bitcast(i32), r[3].bitcast(i32), 0x007FFFFF, 0x3F800000,
                                  ALU.bitwise_and, ALU.bitwise_or).then_inc(mant_ready, 1)
                vec.reciprocal(r[8], r[3])
                vec.tensor_scalar(r[4].bitcast(i32), r[3].bitcast(i32), 23, None,
                                  ALU.logical_shift_right).then_inc(dve_step, 1)
                wait(dve, dve_step, base + 4)
                vec.tensor_tensor(r[8], r[8], zl[:, :, 2], ALU.mult)
                vec.tensor_scalar(r[4], r[4].bitcast(i32), -127.0, LN2, ALU.add, ALU.mult).then_inc(dve_step, 1)
                wait(dve, dve_step, base + 5)
                vec.scalar_tensor_tensor(rows(FA, n), r[8], U_UNIT, rows(At, n), ALU.mult, ALU.mult)
                vec.scalar_tensor_tensor(rows(FC, n), r[8], L_UNIT, rows(Ct, n), ALU.mult, ALU.mult)
                vec.tensor_tensor(r[4], r[4], rows(mthr, n), ALU.add).then_inc(dve_step, 1)

            def row_thresholds(n):
                base = n * ROW_STEPS
                wait(dve, dve_step, base + 6)
                wait(dve, ln_ready, n + 1)
                vec.tensor_tensor(r[9], r[4], r[6], ALU.add).then_inc(dve_step, 1)
                wait(dve, dve_step, base + 7)
                vec.scalar_tensor_tensor(r[10], r[9], 1.0 / SLOPE, r[9], ALU.mult, ALU.min).then_inc(dve_step, 1)
                wait(dve, dve_step, base + 8)
                vec.tensor_tensor(r[11], r[10], sdz[:, 0, ds(n * TB, TB)], ALU.subtract).then_inc(dve_step, 1)

            def scale_rows(k):
                wait(dve, trA_done, k + 1)
                vec.tensor_tensor(E1[:], trA[:].rearrange("p (t f) -> p t f", f=F), over_features(rows(FA, k)),
                                  ALU.mult).then_inc(scaled, 1)
                wait(dve, scaled, k + 1)
                vec.tensor_tensor(E1[:], E1[:], hh[:].rearrange("p (t f) -> p t f", f=F), ALU.add)
                wait(dve, tr_done, k + 1)
                vec.tensor_tensor(E2[:], trC[:].rearrange("p (t f) -> p t f", f=F), over_features(rows(FC, k)),
                                  ALU.mult).then_inc(y_parts, 1)

            def last_y():
                dve.wait_ge(y_parts, NB)
                vec.tensor_tensor(E1[:], E1[:], E2[:], ALU.add).then_inc(ysum, 1)
                dve.wait_ge(ysum, NB)
                vec.tensor_scalar(E2[:], E1[:], 0.0, None, ALU.min).then_inc(y_ready, 1)

            def last_add_x():
                dve.wait_ge(xm_done, NB)
                dve.wait_ge(r_ready, NB)
                vec.tensor_tensor(E1[:], E1[:], xN[:], ALU.add).then_inc(r2_ready, 1)

            def elu(k):
                wait(dve, ex_ready, k + 1)
                vec.scalar_tensor_tensor(E1[:], E1[:], 0.0, E3[:], ALU.max, ALU.add).then_inc(r_ready, 1)

            def norm_stats(k):
                wait(dve, r2_ready, k + 1)
                for t in range(TB):
                    vec.bn_stats(bn[:, t, :], E1[:, t, :]).then_inc(bn_part, 1)
                for t in range(TB):
                    wait(dve, bn_part, k * TB + t + 1)
                    hold(dve)
                    last = vec.bn_aggr(mv[:, t, :], bn[:, t, :])
                last.then_inc(bn_ready, 1)

            def normalise(k):
                wait(dve, rstd_ready, k + 1)
                for t in range(TB):
                    last = vec.tensor_scalar(xN[:, t, :], E1[:, t, :], mv[:, t, 0:1], rstd[:, t:t + 1],
                                             ALU.subtract, ALU.mult)
                last.then_inc(out_ready, 1)

            stage_e = {AT_SCALE: scale_rows, AT_ELU: elu, AT_NORM: norm_stats, AT_OUT: normalise}

            def step(n, par):
                for g in range(NG):
                    ahead, gg = n + 1 + (g + LEAD) // NG, (g + LEAD) % NG
                    par_ahead = (par + (1 if g + LEAD < NG else 0)) % 2
                    if exists(ahead):
                        valid_masks(ahead, gg)
                        upper_chunks(ahead, par_ahead, gg)
                    if exists(n):
                        stage_t(n, par, g)
                    elif g + LEAD < NG:
                        products(g + LEAD)
                    if exists(ahead):
                        branch_masks(ahead, par_ahead, gg)
                    if g in stage_e and exists(n - 1):
                        stage_e[g](n - 1)
                    if g == AT_ROWS_1 and exists(n + 1):
                        row_factors(n + 1)
                    if g == AT_ROWS_2 and exists(n + 1):
                        row_thresholds(n + 1)

            for g in range(LEAD):
                if g >= EARLY:
                    valid_masks(0, g)
                upper_chunks(0, 0, g)
                products(g)
                branch_masks(0, 0, g)
            step(-1, 1)
            all_steps(dve, step)
            scale_rows(NB - 1)
            last_y()
            elu(NB - 1)
            last_add_x()
            norm_stats(NB - 1)
            normalise(NB - 1)

        @block.gpsimd
        def _(pool):
            gp = nc.gpsimd
            gp.memset(a_sb[:, 2:3], 1.0)
            for k, shift in enumerate((SHIFT, SLOPE * SHIFT, -SHIFT, -SLOPE * SHIFT)):
                gp.memset(exp_bias[:, k:k + 1], shift)
            gp.memset(minus_half[:], -0.5)
            gp.memset(WV[:], 0.0)
            gp.memset(WC[:], 0.0).then_inc(setup_done, 1)
            pool.wait_ge(top_ready, 1)
            gp.partition_all_reduce(dmax[:], dtop[:], P, bass.bass_isa.ReduceOp.max).then_inc(max_ready, 1)
            for g in range(NG):
                pool.wait_ge(hi_ready, g + 1)
                for dst, src in ((WB, (E1, E2)[g % 2]), (WD, (E3, xN)[g % 2])):
                    last = gp.tensor_tensor(dst[:, g * CH:(g + 1) * CH, 1, :], src[:],
                                            dst[:, g * CH:(g + 1) * CH, 0, :], ALU.subtract)
                last.then_inc(lo_ready, 1)

            def x_minus_one(k):
                wait(pool, xb_loaded, 32 * (k + 1))
                hold(pool)
                gp.tensor_scalar(xN[:], xN[:], 1.0, None, ALU.subtract).then_inc(xm_done, 1)

            def y_and_sum(k):
                wait(pool, y_parts, k + 1)
                gp.tensor_tensor(E1[:], E1[:], E2[:], ALU.add).then_inc(ysum, 1)
                wait(pool, ysum, k + 1)
                hold(pool)
                gp.tensor_scalar(E2[:], E1[:], 0.0, None, ALU.min).then_inc(y_ready, 1)
                wait(pool, xm_done, k + 1)
                wait(pool, r_ready, k + 1)
                gp.tensor_tensor(E1[:], E1[:], xN[:], ALU.add).then_inc(r2_ready, 1)

            def root(k):
                wait(pool, bn_ready, k + 1)
                hold(pool)
                gp.tensor_scalar(vareps[:], mv[:, :, 1], EPS, None, ALU.add).then_inc(ve_ready, 1)
                wait(pool, ve_ready, k + 1)
                gp.tensor_tensor(rstd[:], vareps[:], minus_half[:], ALU.pow).then_inc(rstd_ready, 1)

            def stage_e(k):
                x_minus_one(k)
                y_and_sum(k)
                root(k)

            stage_e(0)
            with pool.Fori(1, NB - 1) as k:
                stage_e(k)
            x_minus_one(NB - 1)
            root(NB - 1)


def kernel(x, adj, L0_gnn_W, L0_gnn_a):
    import concourse.bacc as bacc
    from concourse.bass_utils import run_bass_kernel_spmd

    x, adj, W, a = (np.ascontiguousarray(v) for v in (x, adj, L0_gnn_W, L0_gnn_a))
    arrays = {
        "x": x,
        "xT": np.ascontiguousarray(x.T),
        "W": W,
        "WT": np.ascontiguousarray(W.T),
        "a_cols": np.ascontiguousarray(a.reshape(2, F).T),
        "adjT": np.ascontiguousarray(
            adj.reshape(NB, BI, NG, 2, CH // 2, P).transpose(0, 2, 5, 3, 4, 1)).reshape(NB, NG, P, 2, HALF),
        "ident": np.eye(P, dtype=np.float32),
    }
    nc = bacc.Bacc("TRN2", target_bir_lowering=False, num_devices=1)
    ins = [nc.dram_tensor(n, v.shape, mybir.dt.from_np(v.dtype), kind="ExternalInput").ap() for n, v in arrays.items()]
    out = nc.dram_tensor("out", (N, F), mybir.dt.float32, kind="ExternalOutput").ap()
    graph_attention(nc, *ins, out)
    return run_bass_kernel_spmd(nc, [arrays], core_ids=[0]).results[0]["out"]
```
